# Optimizing a Trainium2 kernel written in Bass

```python
import numpy as np
import jax
import jax.numpy as jnp

def _softmax(x, axis=-1):
    return jax.nn.softmax(x, axis=axis)

def _gelu(x):
    return jax.nn.gelu(x, approximate=True)

def _silu(x):
    return jax.nn.silu(x)

def _sigmoid(x):
    return jax.nn.sigmoid(x)

def _layernorm(x, axis=-1, eps=1e-05):
    m = jnp.mean(x, axis=axis, keepdims=True)
    v = jnp.var(x, axis=axis, keepdims=True)
    return (x - m) / jnp.sqrt(v + eps)

def _scatter_add(tgt, idx, src, axis=0):
    return tgt.at[idx].add(src)

def _segment_sum(src, seg, n):
    return jax.ops.segment_sum(src, seg, n)
kernel_name = 'mk_prb_d1_jaxref_r8_9fa11b'

def setup_inputs(seed: int=0):
    np.random.seed(seed)
    _w = jnp.asarray

    def _L0_attn_setup():
        import jax, jax.numpy as jnp
        import numpy as np
        import math
        B, S, DIM = (1, 256, 128)
        H, KVH = (16, 4)
        HD = DIM // H
        KV_DIM = KVH * HD

        def _rms_norm(x):
            eps = jnp.finfo(x.dtype).eps
            return x * jax.lax.rsqrt(jnp.mean(x * x, axis=-1, keepdims=True) + eps)

        def _polar_rotary(seq_len, head_dim, dtype):
            angles = jnp.arange(0, head_dim, 2, dtype=jnp.float32) / head_dim * math.pi
            pos = jnp.arange(seq_len, dtype=jnp.float32)
            radius = 1.0 / (1.0 + pos[:, None] * 0.01)
            ang = pos[:, None] * angles[None, :]
            cos = (radius * jnp.cos(ang)).astype(dtype)
            sin = (radius * jnp.sin(ang)).astype(dtype)
            return (cos[None, None], sin[None, None])

        def _apply_rotary(x, cos, sin):
            half = x.shape[-1] // 2
            x1, x2 = (x[..., :half], x[..., half:])
            return jnp.concatenate([x1 * cos + x2 * sin, x1 * -sin + x2 * cos], axis=-1)

        def _causal_attn(q, k, v, scale, mask):
            s = jnp.einsum('bhqd,bhkd->bhqk', q, k) * scale
            s = jnp.where(mask, s, jnp.finfo(s.dtype).min)
            p = jax.nn.softmax(s, axis=-1)
            return jnp.einsum('bhqk,bhkd->bhqd', p, v)
        key = jax.random.key(seed)
        ks = jax.random.split(key, 8)
        std = 0.02
        return {'x': jax.random.normal(ks[0], (B, S, DIM), jnp.float32), 'Wq': jax.random.normal(ks[1], (DIM, DIM), jnp.float32) * std, 'Wk': jax.random.normal(ks[2], (KV_DIM, DIM), jnp.float32) * std, 'Wv': jax.random.normal(ks[3], (KV_DIM, DIM), jnp.float32) * std, 'Wg': jax.random.normal(ks[4], (KV_DIM, DIM), jnp.float32) * std, 'Wo': jax.random.normal(ks[5], (DIM, DIM), jnp.float32) * std, 'q_gain': jnp.full((H,), 1.0, jnp.float32), 'lambda_param': jnp.full((H,), 0.5, jnp.float32)}
    _L0_attn_in = _L0_attn_setup()

    def _L0_ffn_setup():
        import jax, jax.numpy as jnp
        import numpy as np
        E = 8
        D = 128
        H = 256
        TOP_K = 2
        key = jax.random.key(seed)
        k_x, k_g, k_w1, k_w2 = jax.random.split(key, 4)
        B, S = (4, 256)
        inp = {'input': jax.random.normal(k_x, (B, S, D), dtype=jnp.float32), 'Wg': jax.random.normal(k_g, (D, E), dtype=jnp.float32) * 0.02, 'W1': jax.random.normal(k_w1, (E, D, H), dtype=jnp.float32) * 0.02, 'b1': jnp.zeros((E, H), dtype=jnp.float32), 'W2': jax.random.normal(k_w2, (E, H, D), dtype=jnp.float32) * 0.02, 'b2': jnp.zeros((E, D), dtype=jnp.float32)}
        return inp
    _L0_ffn_in = _L0_ffn_setup()
    _d = {'L0_attn_x': _L0_attn_in['x'], 'L0_attn_Wq': _L0_attn_in['Wq'], 'L0_attn_Wk': _L0_attn_in['Wk'], 'L0_attn_Wv': _L0_attn_in['Wv'], 'L0_attn_Wg': _L0_attn_in['Wg'], 'L0_attn_Wo': _L0_attn_in['Wo'], 'L0_attn_q_gain': _L0_attn_in['q_gain'], 'L0_attn_lambda_param': _L0_attn_in['lambda_param'], 'L0_ffn_Wg': _L0_ffn_in['Wg'], 'L0_ffn_W1': _L0_ffn_in['W1'], 'L0_ffn_b1': _L0_ffn_in['b1'], 'L0_ffn_W2': _L0_ffn_in['W2'], 'L0_ffn_b2': _L0_ffn_in['b2']}
    _x0 = _d['L0_attn_x']
    _d['L0_attn_x'] = jax.random.normal(jax.random.fold_in(jax.random.key(seed), 1), (32, 256, 128), dtype=_x0.dtype)
    del _x0
    return _d

def reference(L0_attn_x, L0_attn_Wq, L0_attn_Wk, L0_attn_Wv, L0_attn_Wg, L0_attn_Wo, L0_attn_q_gain, L0_attn_lambda_param, L0_ffn_Wg, L0_ffn_W1, L0_ffn_b1, L0_ffn_W2, L0_ffn_b2):

    def _L0_attn_ref(x, Wq, Wk, Wv, Wg, Wo, q_gain, lambda_param):
        import jax, jax.numpy as jnp
        import numpy as np
        import math
        B, S, DIM = (1, 256, 128)
        H, KVH = (16, 4)
        HD = DIM // H
        KV_DIM = KVH * HD

        def _rms_norm(x):
            eps = jnp.finfo(x.dtype).eps
            return x * jax.lax.rsqrt(jnp.mean(x * x, axis=-1, keepdims=True) + eps)

        def _polar_rotary(seq_len, head_dim, dtype):
            angles = jnp.arange(0, head_dim, 2, dtype=jnp.float32) / head_dim * math.pi
            pos = jnp.arange(seq_len, dtype=jnp.float32)
            radius = 1.0 / (1.0 + pos[:, None] * 0.01)
            ang = pos[:, None] * angles[None, :]
            cos = (radius * jnp.cos(ang)).astype(dtype)
            sin = (radius * jnp.sin(ang)).astype(dtype)
            return (cos[None, None], sin[None, None])

        def _apply_rotary(x, cos, sin):
            half = x.shape[-1] // 2
            x1, x2 = (x[..., :half], x[..., half:])
            return jnp.concatenate([x1 * cos + x2 * sin, x1 * -sin + x2 * cos], axis=-1)

        def _causal_attn(q, k, v, scale, mask):
            s = jnp.einsum('bhqd,bhkd->bhqk', q, k) * scale
            s = jnp.where(mask, s, jnp.finfo(s.dtype).min)
            p = jax.nn.softmax(s, axis=-1)
            return jnp.einsum('bhqk,bhkd->bhqd', p, v)
        bsz, seqlen, dim = x.shape
        q = (x @ Wq.T).reshape(bsz, seqlen, H, HD).transpose(0, 2, 1, 3)
        k = (x @ Wk.T).reshape(bsz, seqlen, KVH, HD).transpose(0, 2, 1, 3)
        v = (x @ Wv.T).reshape(bsz, seqlen, KVH, HD).transpose(0, 2, 1, 3)
        v_g = jax.nn.sigmoid((x @ Wg.T).reshape(bsz, seqlen, KVH, HD).transpose(0, 2, 1, 3))
        v = v * v_g
        q = _rms_norm(q)
        k = _rms_norm(k)
        cos, sin = _polar_rotary(seqlen, HD, q.dtype)
        q = _apply_rotary(q, cos, sin)
        k = _apply_rotary(k, cos, sin)
        q = q * q_gain.astype(q.dtype)[None, :, None, None]
        rep = H // KVH
        k = jnp.repeat(k, rep, axis=1)
        v = jnp.repeat(v, rep, axis=1)
        half = HD // 2
        q1, q2 = (q[..., :half], q[..., half:])
        k1, k2 = (k[..., :half], k[..., half:])
        v1, v2 = (v[..., :half], v[..., half:])
        scale = 1.0 / math.sqrt(half)
        mask = jnp.tril(jnp.ones((seqlen, seqlen), dtype=bool))[None, None]
        a1 = _causal_attn(q1, k1, v1, scale, mask)
        a2 = _causal_attn(q2, k2, v2, scale, mask)
        lp = lambda_param.astype(q.dtype)[None, :, None, None]
        y = jnp.concatenate([a1 - lp * a2, a1 + lp * a2], axis=-1)
        y = y.transpose(0, 2, 1, 3).reshape(bsz, seqlen, dim)
        return y @ Wo.T

    def _L0_ffn_ref(input, Wg, W1, b1, W2, b2):
        import jax, jax.numpy as jnp
        import numpy as np
        E = 8
        D = 128
        H = 256
        TOP_K = 2
        logits = jnp.einsum('bsd,de->bse', input, Wg)
        probs = jax.nn.softmax(logits, axis=-1)
        top_vals, top_idx = jax.lax.top_k(probs, TOP_K)
        top_vals = top_vals / jnp.sum(top_vals, axis=-1, keepdims=True)
        onehot = jax.nn.one_hot(top_idx, E, dtype=input.dtype)
        mask = jnp.sum(onehot, axis=2)
        scores = jnp.sum(onehot * top_vals[..., None], axis=2)
        xm = input[None] * jnp.moveaxis(mask, -1, 0)[..., None]
        h = jnp.einsum('ebsd,edh->ebsh', xm, W1) + b1[:, None, None, :]
        h = jax.nn.relu(h)
        y = jnp.einsum('ebsh,ehd->ebsd', h, W2) + b2[:, None, None, :]
        out = jnp.sum(y * jnp.moveaxis(scores, -1, 0)[..., None], axis=0)
        return out
    x = L0_attn_x
    xn = _layernorm(x, axis=-1)
    x = x + _L0_attn_ref(xn, L0_attn_Wq, L0_attn_Wk, L0_attn_Wv, L0_attn_Wg, L0_attn_Wo, L0_attn_q_gain, L0_attn_lambda_param) + _L0_ffn_ref(xn, L0_ffn_Wg, L0_ffn_W1, L0_ffn_b1, L0_ffn_W2, L0_ffn_b2)
    return x

_drawn_inputs = setup_inputs


def setup_inputs(seed=0):
    import zlib

    import numpy as np

    out = dict(_drawn_inputs(seed))
    spreads = {'L0_attn_q_gain': (1.0, 0.6),
     'L0_attn_lambda_param': (0.5, 0.6),
     'L0_ffn_b1': (0.0, 0.53),
     'L0_ffn_b2': (0.0, 0.1)}
    factors = {'L0_attn_Wq': 8.0,
     'L0_attn_Wk': 8.0,
     'L0_attn_Wv': 8.0,
     'L0_attn_Wg': 8.0,
     'L0_attn_Wo': 8.0}
    for name, (base, spread) in spreads.items():
        noise = np.random.default_rng([zlib.crc32(name.encode()), seed]).standard_normal(out[name].shape)
        drawn = base * np.exp(spread * noise) if base else spread * noise
        out[name] = jnp.asarray(drawn.astype(out[name].dtype))
    for name, factor in factors.items():
        out[name] = (out[name] * factor).astype(out[name].dtype)
    return out
```

```python
import math
from contextlib import ExitStack

import numpy as np

import concourse.bass as bass
from concourse import mybir

F32 = mybir.dt.float32
F16 = mybir.dt.float16
BF16 = mybir.dt.bfloat16
I32 = mybir.dt.int32
U32 = mybir.dt.uint32
ALU = mybir.AluOpType
ACT = mybir.ActivationFunctionType
AX = mybir.AxisListType

P = 128
NB, S, D = 32, 256, 128
T = S // P
H, KVH = 16, 4
HD = D // H
HALF = HD // 2
REP = H // KVH
KV = KVH * HD
GF = KVH * 2
NE, HID = 8, 256
HC = HID // P
NPROJ = D + 3 * KV + NE
QKH = H + KVH
UNITS = 12
UW = 1024
RING = 4
LN_EPS = 1e-5
RMS_EPS = float(np.finfo(np.float32).eps)
SCALE = 1.0 / math.sqrt(HALF)
GAIN_LIMIT = 8.0
NEG = -3.0e38

_stages = {
    "STATS": T, "VAR_IN": 1 + T, "VAR": 1, "XN": T, "SQUARES": 1 + T, "SUMS": 1 + T, "MS": 1, "LDIFF": 1, "TOPF": 1,
    "DEN": 2, "WTOP0": 2, "WTOP1": 1, "ONEHOT": 2 * T, "SCORE": 1, "RG": 1, "XR": 1, "ROT": 3, "QKF": T + 1,
    "HIGH": 2, "QP": 1, "KP": 1,
}
PREP = dict(zip(_stages, (int(n) for n in np.cumsum(list(_stages.values())))))
PREP_STEPS = PREP["KP"]
TAIL_STEPS = 1
SETUP_STEPS = 34
WEIGHTS = 14 * 16

UNIT = []
for _f in range(2):
    for _pair in range(KVH // 2):
        _g = 2 * _pair
        UNIT += [(_f, 0, (_g,)), (_f, 0, (_g + 1,)), (_f, 1, (_g, _g + 1))]
assert len(UNIT) == UNITS

TAIL_PVT, TAIL_AT, TAIL_OUT = 0, 1, 2
PREP_XNT, PREP_PROJ, PREP_ST, PREP_QT, PREP_KT = 3, 4, 7, 9, 10
MISC_PER_SEQ = 8
ROUNDS = 12


def at(b, per, k):
    return (2 * per) * b[0] + (per * b[1] + k)


def after(b):
    return b[0] + b[1], 1 - b[1]


def before(b):
    return b[0] - (1 - b[1]), 1 - b[1]


def moe_attention_kernel(nc, x, w_proj, wo_a, wo_b, gain, lam_col, w1, b1, w2, b2, cos_t, sin_t, gf_mask, ident, causal_neg, out):
    ctx = ExitStack()
    with ctx:
        def sb(name, shape, dt=F32):
            return ctx.enter_context(nc.sbuf_tensor(name, shape, dt))

        def pb(name, shape, dt=F32):
            return ctx.enter_context(nc.psum_tensor(name, shape, dt))

        def sem(name):
            return ctx.enter_context(nc.semaphore(name))

        wproj_sb = sb("wproj_sb", [P, NPROJ])
        woa_sb = sb("woa_sb", [P, D])
        wob_sb = sb("wob_sb", [P, D])
        wo_sb = sb("wo_sb", [P, D])
        lamc = sb("lamc", [P, 1])
        lamn = sb("lamn", [P, 1])
        w1_sb = sb("w1_sb", [P, NE, HID])
        b1_sb = sb("b1_sb", [P, NE, HC])
        w2_sb = sb("w2_sb", [P, NE, HC, D])
        b2_sb = sb("b2_sb", [NE, D])
        cos_sb = sb("cos_sb", [P, T, HD])
        sin_sb = sb("sin_sb", [P, T, HD])
        gfm_sb = sb("gfm_sb", [P, GF])
        id32 = sb("id32", [P, P])
        id16 = sb("id16", [P, P], F16)
        idb = sb("idb", [P, P], BF16)
        neg32 = sb("neg32", [P, P])
        negb = sb("negb", [P, P], BF16)
        gain_sb = sb("gain_sb", [P, H])
        gabs = sb("gabs", [P, H])
        gmax = sb("gmax", [P, 1])
        big = sb("big", [P, 1])
        big_i = sb("big_i", [P, 1], I32)
        gsgn = sb("gsgn", [P, H])
        gtmp = sb("gtmp", [P, H])
        qmul = sb("qmul", [P, T, QKH])
        iota8 = sb("iota8", [P, NE])
        mhalf = sb("mhalf", [P, T * QKH])

        xs = [sb(f"xs{i}", [P, T, D]) for i in range(2)]
        stats = sb("stats", [P, T, 6])
        mv = sb("mv", [P, T, 2])
        vare = sb("vare", [P, T])
        rstd = sb("rstd", [P, T])
        xn = sb("xn", [P, T, D])
        xnT = [sb(f"xnT{i}", [P, S]) for i in range(2)]
        proj = sb("proj", [P, T, NPROJ])
        sq = sb("sq", [P, T, QKH * HD])
        ms = sb("ms", [P, T * QKH])
        rinv = sb("rinv", [P, T * QKH])
        rg = sb("rg", [P, T * QKH])
        xr = sb("xr", [P, T, QKH, HD])
        ra = sb("ra", [P, T, QKH, HD])
        rb = sb("rb", [P, T, QKH, HD])
        qf = sb("qf", [P, T, REP, KVH, HD])
        kf = sb("kf", [P, T, KVH, HD])
        qp = sb("qp", [P, T, REP, GF, 4, HALF], F16)
        kp = sb("kp", [P, T, GF, 4, HALF], F16)
        qT = [sb(f"qT{i}", [P, REP, S], F16) for i in range(2)]
        kT = sb("kT", [P, S], F16)
        kpad = [sb(f"kpad{i}", [P, GF, S], F16) for i in range(2)]
        egate = sb("egate", [P, T, KV])
        gden = sb("gden", [P, T, KV])
        gsig = sb("gsig", [P, T, KV])
        vw = [sb(f"vw{i}", [P, 2 * GF * 32 + 32]) for i in range(2)]
        top = sb("top", [P, T, 8])
        topi = sb("topi", [P, T, 8], U32)
        topf = sb("topf", [P, T, 2])
        ldiff = sb("ldiff", [P, T])
        eldiff = sb("eldiff", [P, T])
        wden = sb("wden", [P, T])
        wtop = sb("wtop", [P, 2, T])
        s0 = sb("s0", [P, T, NE])
        s1 = sb("s1", [P, T, NE])
        score = [sb(f"score{i}", [P, T, NE]) for i in range(2)]
        scoreT = [sb(f"scoreT{i}", [NE, S]) for i in range(2)]
        probs = [sb(f"probs{i}", [P, UW]) for i in range(RING)]
        hT = [sb(f"hT{i}", [P, HC, S]) for i in range(2)]
        acc = [sb(f"acc{i}", [P, T, D]) for i in range(2)]
        pvs = sb("pvs", [P, 2, S])
        pinv = sb("pinv", [P, 64])
        an = sb("an", [P, T, D])
        aT = sb("aT", [P, S])
        ofin = [sb(f"ofin{i}", [P, T, D]) for i in range(2)]
        nmax = sb("nmax", [P, T, 32])
        nmaxT = sb("nmaxT", [32, S])
        credits = sb("credits", [P, 16])
        hold = sb("hold", [P, 1])

        sbank = [pb(f"sbank{i}", [P, UW]) for i in range(2)]
        pvbank = pb("pvbank", [P, 2, S])
        hbank = pb("hbank", [P, HC, S])
        ybank = pb("ybank", [P, 512])
        misc = pb("misc", [P, 512])
        misc16 = misc[:, :].bitcast(F16)

        def vw_view(p, kb, c0, c1):
            flat = vw[p][:, kb * 256:kb * 256 + 288].rearrange("p (g x) -> p g x", g=KVH)
            return flat[:, :, 0:64].rearrange("p g (f y) -> p g f y", f=2)[:, :, :, c0:c1]

        weights_in = sem("weights_in")
        x_in = [sem(f"x_in{i}") for i in range(2)]
        out_stored = [sem(f"out_stored{i}") for i in range(2)]
        setup = sem("setup")
        prep_step = sem("prep_step")
        tail_step = sem("tail_step")
        ln_rstd = sem("ln_rstd")
        rms_inv = sem("rms_inv")
        prep_exp = sem("prep_exp")
        v_ready = sem("v_ready")
        k_ready = sem("k_ready")
        xnT_psum = sem("xnT_psum")
        proj_psum = sem("proj_psum")
        sT_psum = sem("sT_psum")
        qT_psum = sem("qT_psum")
        kT_psum = sem("kT_psum")
        pvT_psum = sem("pvT_psum")
        aT_psum = sem("aT_psum")
        attn_psum = sem("attn_psum")
        misc_evacuated = sem("misc_evacuated")
        scores_ready = sem("scores_ready")
        exp_done = [sem(f"exp_done{i}") for i in range(RING)]
        mask_done = sem("mask_done")
        pv_done = sem("pv_done")
        pv_evacuated = sem("pv_evacuated")
        h_psum = sem("h_psum")
        relu_done = sem("relu_done")
        y_psum = sem("y_psum")
        comb_done = sem("comb_done")
        max_psum = sem("max_psum")
        max_read = sem("max_read")

        block = ctx.enter_context(nc.Block())

        def misc_turn(b, k, past=False):
            order = [TAIL_PVT, TAIL_AT, TAIL_OUT, PREP_XNT, PREP_PROJ, PREP_ST, PREP_QT, PREP_KT]
            n = order.index(k)
            return n - 3 if b is None else at(b, MISC_PER_SEQ, 5 + n if past else 2 + n)

        def schedule(eng, seq):
            a, z = (0, 0), (0, 1)
            seq(a, z, None)
            seq(z, after(z), a)
            with eng.Fori(1, NB // 2 - 1) as i:
                for p in range(2):
                    b = (i, p)
                    seq(b, after(b), before(b))
            a, z = (NB // 2 - 1, 0), (NB // 2 - 1, 1)
            seq(a, z, before(a))
            seq(z, None, a)
            return z

        @block.sync
        def _(sp):
            xr_ = x.rearrange("b (t p) d -> b p t d", p=P)
            or_ = out.rearrange("b (t p) d -> b p t d", p=P)
            sp.dma_start(xs[0][:], xr_[0]).then_inc(x_in[0], 16)
            for dst, src in ((wproj_sb[:], w_proj), (id32[:], ident), (gain_sb[:], gain), (cos_sb[:], cos_t),
                             (sin_sb[:], sin_t), (gfm_sb[:], gf_mask), (neg32[:], causal_neg),
                             (woa_sb[:], wo_a), (wob_sb[:], wo_b), (lamc[:], lam_col), (b1_sb[:], b1),
                             (b2_sb[:], b2), (w1_sb[:], w1), (w2_sb[:], w2)):
                sp.dma_start(dst, src).then_inc(weights_in, 16)
            sp.dma_start(xs[1][:], xr_[1]).then_inc(x_in[1], 16)

            def store(b, turn):
                sp.wait_ge(misc_evacuated, turn + 2)
                sp.dma_start(or_[2 * b[0] + b[1]], ofin[b[1]][:]).then_inc(out_stored[b[1]], 16)

            def seq(b, nxt, prv):
                if prv is not None:
                    store(prv, misc_turn(b, TAIL_OUT))
                if not (isinstance(b[0], int) and b[0] == NB // 2 - 1):
                    sp.wait_ge(comb_done, at(b, NE, 2))
                    sp.dma_start(xs[b[1]][:], xr_[2 * b[0] + (b[1] + 2)]).then_inc(x_in[b[1]], 16)

            last = schedule(sp, seq)
            store(last, misc_turn(last, TAIL_OUT, past=True))
            for p in range(2):
                sp.wait_ge(out_stored[p], 16 * (NB // 2 + 1))

        @block.tensor
        def _(pe):
            def xn_transposes(b, turn):
                pe.wait_ge(misc_evacuated, turn + 1)
                pe.wait_ge(prep_step, at(b, PREP_STEPS, PREP["XN"]))
                for t in range(T):
                    last = pe.transpose(misc[:, t * P:(t + 1) * P], xn[:, t, :], id32[:])
                last.then_inc(xnT_psum, 1)

            def projection(b, turn):
                pe.wait_ge(misc_evacuated, turn + 1)
                for t in range(T):
                    last = pe.matmul(misc[:, t * NPROJ:(t + 1) * NPROJ], xnT[b[1]][:, t * P:(t + 1) * P],
                                     wproj_sb[:], start=True, stop=True)
                last.then_inc(proj_psum, 1)

            def score_transposes(b, turn):
                pe.wait_ge(misc_evacuated, turn + 1)
                pe.wait_ge(prep_step, at(b, PREP_STEPS, PREP["SCORE"]))
                for t in range(T):
                    last = pe.transpose(misc[0:NE, t * P:(t + 1) * P], score[b[1]][:, t, :], id32[:])
                last.then_inc(sT_psum, 1)

            def q_transposes(b, turn):
                pe.wait_ge(misc_evacuated, turn + 1)
                pe.wait_ge(prep_step, at(b, PREP_STEPS, PREP["QP"]))
                for r in range(REP):
                    for t in range(T):
                        o = (r * T + t) * P
                        last = pe.transpose(misc16[:, o:o + P], qp[:, t, r].rearrange("p a b c -> p (a b c)"), id16[:])
                last.then_inc(qT_psum, 1)

            def k_transposes(b, turn):
                pe.wait_ge(misc_evacuated, turn + 1)
                pe.wait_ge(prep_step, at(b, PREP_STEPS, PREP["KP"]))
                for t in range(T):
                    last = pe.transpose(misc16[:, t * P:(t + 1) * P], kp[:, t].rearrange("p a b c -> p (a b c)"), id16[:])
                last.then_inc(kT_psum, 1)

            def pv_transposes(b, turn):
                pe.wait_ge(misc_evacuated, turn + 1)
                pe.wait_ge(pv_evacuated, at(b, 1, 2))
                for t in range(T):
                    for f in range(2):
                        o = (t * 2 + f) * P
                        last = pe.transpose(misc[:, o:o + P], pvs[:, f, t * P:(t + 1) * P], id32[:])
                last.then_inc(pvT_psum, 1)

            def a_transposes(b, turn):
                pe.wait_ge(misc_evacuated, turn + 1)
                for t in range(T):
                    last = pe.transpose(misc[:, t * P:(t + 1) * P], an[:, t, :], id32[:])
                last.then_inc(aT_psum, 1)

            def attention_out(b, turn):
                pe.wait_ge(misc_evacuated, turn + 1)
                for t in range(T):
                    o = misc[:, t * P:(t + 1) * P]
                    pe.matmul(o, aT[:, t * P:(t + 1) * P], wo_sb[:], start=True, stop=False)
                    last = pe.matmul(o, scoreT[b[1]][:, t * P:(t + 1) * P], b2_sb[:], start=False, stop=True)
                last.then_inc(attn_psum, 1)

            def score_unit(b, u, general):
                f, kb, gs = UNIT[u]
                bank = sbank[u % 2]
                for n in range(2):
                    if kb == 0:
                        rhs, g = qT[b[1]][:, 2 * n:2 * n + 2, :], gs[0]
                    else:
                        rhs, g = qT[b[1]][:, :, P:S], gs[n]
                    gf = 2 * g + f
                    o = bank[:, n * 512:(n + 1) * 512]
                    last = pe.matmul(o, kpad[b[1]][:, gf, kb * P:(kb + 1) * P], rhs, start=True, stop=not general,
                                     skip_group_check=general)
                    if general:
                        heads = (2 * n, 2 * n + 1) if kb == 0 else range(REP)
                        w = S // (kb + 1)
                        for j, r in enumerate(heads):
                            hh = gf * REP + r
                            last = pe.matmul(o[:, j * w:(j + 1) * w], id32[0:32, hh:hh + 1].to_broadcast([32, P]),
                                             nmaxT[:, kb * P:S], start=False, stop=True, skip_group_check=True)
                last.then_inc(scores_ready, 1)

            def scores(b, u):
                pe.wait_ge(mask_done, at(b, UNITS, u + 1))
                if u == 0:
                    pe.wait_ge(k_ready, at(b, GF, GF))
                with pe.If(general_path):
                    score_unit(b, u, True)
                with pe.Else():
                    score_unit(b, u, False)

            def exact_maxima(b, current):
                with pe.If(general_path):
                    pe.wait_ge(k_ready, at(b, GF, GF))
                    if current is not None:
                        pe.wait_ge(mask_done, at(current, UNITS, UNITS + 1))
                    for n in range(ROUNDS):
                        pe.wait_ge(max_read, at(b, ROUNDS + 1, n + 1))
                        t, gfs = (0, (2 * n, 2 * n + 1)) if n < 4 else (1, (n - 4,))
                        w = (t + 1) * P
                        for j, gf in enumerate(gfs):
                            for r in range(REP):
                                o = sbank[0][:, (j * REP + r) * w:(j * REP + r + 1) * w]
                                pe.matmul(o, qT[b[1]][:, r, t * P:(t + 1) * P], kpad[b[1]][:, gf, 0:w],
                                          start=True, stop=False, skip_group_check=True)
                                last = pe.matmul(o[:, t * P:w], idb[:], negb[:], start=False, stop=True,
                                                 skip_group_check=True)
                        last.then_inc(max_psum, 1)
                    pe.wait_ge(max_read, at(b, ROUNDS + 1, ROUNDS + 1))
                    for t in range(T):
                        last = pe.transpose(sbank[0][0:32, t * P:(t + 1) * P], nmax[:, t, :], id32[:])
                    last.then_inc(max_psum, 1)
                    pe.wait_ge(max_read, at(b, ROUNDS + 1, ROUNDS + 2))

            def values(b, u):
                f, kb, gs = UNIT[u]
                pe.wait_ge(mask_done, at(b, UNITS, u + 3))
                if u == 0:
                    pe.wait_ge(v_ready, at(b, 2, 2))
                    pe.wait_ge(pv_evacuated, at(b, 1, 1))
                for n, g in enumerate(gs):
                    gf = 2 * g + f
                    for r in range(REP):
                        w = S // (kb + 1)
                        rhs = probs[u % RING][:, (n * REP + r) * w:(n * REP + r + 1) * w]
                        last = pe.matmul(pvbank[32 * r:32 * r + 32, f, kb * P:S],
                                         vw[b[1]][:, (kb * GF + gf) * 32:(kb * GF + gf + 1) * 32], rhs,
                                         start=(g == 0 and kb == 0), stop=(g == KVH - 1 and kb == 1),
                                         skip_group_check=True)
                last.then_inc(pv_done, 1)

            def expert_in(b, e):
                pe.wait_ge(relu_done, at(b, NE, e + 1))
                for c in range(HC):
                    last = pe.matmul(hbank[:, c, :], w1_sb[:, e, c * P:(c + 1) * P], xnT[b[1]][:],
                                     start=True, stop=True)
                last.then_inc(h_psum, 1)

            def expert_out(b, e):
                pe.wait_ge(relu_done, at(b, NE, e + 2))
                pe.wait_ge(comb_done, at(b, NE, e + 1))
                for t in range(T):
                    for c in range(HC):
                        last = pe.matmul(ybank[:, t * P:(t + 1) * P], hT[e % 2][:, c, t * P:(t + 1) * P],
                                         w2_sb[:, e, c, :], start=(c == 0), stop=(c == HC - 1))
                last.then_inc(y_psum, 1)

            def seq(b, nxt, prv):
                for u in range(UNITS):
                    if u < UNITS - 1:
                        scores(b, u + 1)
                    elif nxt is not None:
                        exact_maxima(nxt, b)
                        scores(nxt, 0)
                    if u < NE:
                        expert_in(b, u)
                    if 1 <= u <= NE:
                        expert_out(b, u - 1)
                    if prv is not None:
                        for k, step in ((TAIL_PVT, pv_transposes), (TAIL_AT, a_transposes), (TAIL_OUT, attention_out)):
                            if u == k:
                                step(prv, misc_turn(b, k))
                    if nxt is not None:
                        for k, step in prep_steps:
                            if u == k:
                                step(nxt, misc_turn(b, k))
                    values(b, u)

            prep_steps = ((PREP_XNT, xn_transposes), (PREP_PROJ, projection), (PREP_ST, score_transposes),
                    (PREP_QT, q_transposes), (PREP_KT, k_transposes))
            pe.wait_ge(weights_in, WEIGHTS)
            pe.wait_ge(setup, SETUP_STEPS)
            general_path = pe.value_load(big_i[0:1, 0:1], min_val=0, max_val=1)
            first = (0, 0)
            for k, step in prep_steps:
                step(first, misc_turn(None, k))
            exact_maxima(first, None)
            scores(first, 0)
            last = schedule(pe, seq)
            for k, step in ((TAIL_PVT, pv_transposes), (TAIL_AT, a_transposes), (TAIL_OUT, attention_out)):
                step(last, misc_turn(last, k, past=True))

        @block.scalar
        def _(act):
            def exps(b, u):
                def ready():
                    act.wait_ge(pv_done, at(b, UNITS, u + 1))
                    act.wait_ge(scores_ready, at(b, UNITS, u + 1))
                f, kb, gs = UNIT[u]
                dst, src = probs[u % RING], sbank[u % 2]
                with act.If(general_path):
                    ready()
                    w = S // (kb + 1)
                    for n, g in enumerate(gs):
                        for r in range(REP):
                            a, h = (n * REP + r) * w, g * REP + r
                            last = nc.scalar.activation(dst[:, a:a + w], src[:, a:a + w], ACT.Exp,
                                                        scale=gabs[:, h:h + 1])
                    last.then_inc(exp_done[u % RING], 1)
                with act.Else():
                    ready()
                    nc.scalar.activation(dst[:], src[:], ACT.Exp).then_inc(exp_done[u % RING], 1)

            def relus(b, e):
                act.wait_ge(h_psum, at(b, NE, e + 1))
                act.wait_ge(y_psum, at(b, NE, e + 1))
                for c in range(HC):
                    last = nc.scalar.activation(hT[e % 2][:, c, :], hbank[:, c, :], ACT.Relu,
                                                bias=b1_sb[:, e, c:c + 1])
                last.then_inc(relu_done, 1)

            def prep_exps(b):
                act.wait_ge(prep_step, at(b, PREP_STEPS, PREP["LDIFF"]))
                nc.scalar.activation(egate[:], proj[:, :, D + 2 * KV:D + 3 * KV], ACT.Exp, scale=-1.0)
                nc.scalar.activation(eldiff[:], ldiff[:], ACT.Exp).then_inc(prep_exp, 1)

            def seq(b, nxt, prv):
                for u in range(UNITS):
                    exps(b, u)
                    if u < NE:
                        relus(b, u)
                    if u == 6 and nxt is not None:
                        prep_exps(nxt)

            act.wait_ge(weights_in, WEIGHTS)
            act.wait_ge(setup, SETUP_STEPS)
            general_path = act.value_load(big_i[0:1, 0:1], min_val=0, max_val=1)
            prep_exps((0, 0))
            schedule(act, seq)

        @block.gpsimd
        def _(pool):
            def masks(b, u):
                f, kb, gs = UNIT[u]
                pool.wait_ge(exp_done[u % RING], 1)
                pool.sem_clear(exp_done[u % RING])
                if kb == 0:
                    v = probs[u % RING][:].rearrange("p (r q) -> p r q", r=REP)[:, :, 0:P]
                    n = REP
                else:
                    v = probs[u % RING][:].rearrange("p (r q) -> p r q", r=2 * REP)
                    n = 2 * REP
                nc.gpsimd.affine_select(out=v, in_=v, compare_op=ALU.is_ge, fill=0.0, base=0,
                                        pattern=[[0, n], [1, P]], channel_multiplier=-1).then_inc(mask_done, 1)

            def layer_rstd(b):
                pool.wait_ge(prep_step, at(b, PREP_STEPS, PREP["VAR"]))
                nc.gpsimd.tensor_tensor(rstd[:], vare[:], mhalf[:, 0:T], ALU.pow).then_inc(ln_rstd, 1)

            def head_rms(b):
                pool.wait_ge(prep_step, at(b, PREP_STEPS, PREP["MS"]))
                nc.gpsimd.tensor_tensor(rinv[:], ms[:], mhalf[:], ALU.pow).then_inc(rms_inv, 1)

            def seq(b, nxt, prv):
                for u in range(UNITS):
                    masks(b, u)
                    if u == 0 and nxt is not None:
                        layer_rstd(nxt)
                    if u == 5 and nxt is not None:
                        head_rms(nxt)

            pool.wait_ge(setup, SETUP_STEPS)
            layer_rstd((0, 0))
            head_rms((0, 0))
            schedule(pool, seq)

        @block.vector
        def _(dve):
            dve.wait_ge(weights_in, WEIGHTS)
            dve.tensor_copy(id16[:], id32[:]).then_inc(setup, 1)
            dve.tensor_copy(idb[:], id32[:]).then_inc(setup, 1)
            dve.tensor_copy(negb[:], neg32[:]).then_inc(setup, 1)
            dve.memset(mhalf[:], -0.5).then_inc(setup, 1)
            for j in range(NE):
                dve.memset(iota8[:, j:j + 1], float(j)).then_inc(setup, 1)
            for p in range(2):
                dve.memset(vw[p][:], 0.0).then_inc(setup, 1)
            dve.wait_ge(setup, 14)
            for p in range(2):
                for kb in range(2):
                    dve.memset(vw_view(p, kb, HALF, HALF + 1), 1.0).then_inc(setup, 1)
            dve.tensor_scalar(gtmp[:], gain_sb[:], -1.0, None, ALU.mult).then_inc(setup, 1)
            dve.wait_ge(setup, 19)
            dve.tensor_tensor(gabs[:], gtmp[:], gain_sb[:], ALU.max).then_inc(setup, 1)
            dve.wait_ge(setup, 20)
            dve.tensor_reduce(gmax[:], gabs[:], AX.X, ALU.max).then_inc(setup, 1)
            dve.tensor_scalar(gsgn[:], gain_sb[:], 0.0, 2.0, ALU.is_ge, ALU.mult).then_inc(setup, 1)
            dve.wait_ge(setup, 22)
            dve.tensor_scalar(big[:], gmax[:], GAIN_LIMIT, None, ALU.is_gt).then_inc(setup, 1)
            dve.scalar_tensor_tensor(out=gtmp[:], in0=gsgn[:], scalar=-1.0, in1=gain_sb[:], op0=ALU.add, op1=ALU.subtract).then_inc(setup, 1)
            dve.wait_ge(setup, 24)
            dve.tensor_copy(big_i[:], big[:]).then_inc(setup, 1)
            dve.scalar_tensor_tensor(out=gsgn[:], in0=gtmp[:], scalar=big[:, 0:1], in1=gain_sb[:], op0=ALU.mult, op1=ALU.add).then_inc(setup, 1)
            dve.wait_ge(setup, 26)
            for t in range(T):
                dve.tensor_scalar(qmul[:, t, 0:H], gsgn[:], SCALE, None, ALU.mult).then_inc(setup, 1)
                dve.memset(qmul[:, t, H:QKH], 1.0).then_inc(setup, 1)
            dve.tensor_scalar(lamn[0:64, :], lamc[0:64, :], 1.0, None, ALU.mult).then_inc(setup, 1)
            dve.tensor_scalar(lamn[64:P, :], lamc[64:P, :], -1.0, None, ALU.mult).then_inc(setup, 1)
            dve.wait_ge(setup, 32)
            dve.tensor_scalar(wo_sb[:], woa_sb[:], lamn[:, 0:1], None, ALU.mult).then_inc(setup, 1)
            dve.wait_ge(setup, 33)
            dve.scalar_tensor_tensor(out=wo_sb[:], in0=wob_sb[:], scalar=lamc[:, 0:1], in1=wo_sb[:], op0=ALU.mult, op1=ALU.add).then_inc(setup, 1)
            dve.wait_ge(setup, SETUP_STEPS)
            n_credit = 0
            for s, v in ((misc_evacuated, 1), (mask_done, 2), (pv_done, RING), (pv_evacuated, 1), (relu_done, 1),
                         (y_psum, 2), (comb_done, 1), (max_read, 1), (out_stored[0], 16), (out_stored[1], 16)):
                dve.memset(credits[:, n_credit:n_credit + 1], 0.0).then_inc(s, v)
                n_credit += 1

            def ln_stats(b):
                dve.wait_ge(x_in[b[1]], 16 * b[0] + 16)
                for t in range(T):
                    dve.bn_stats(stats[:, t, :], xs[b[1]][:, t, :]).then_inc(prep_step, 1)
                dve.wait_ge(prep_step, at(b, PREP_STEPS, PREP["STATS"]))
                dve.memset(hold[:], 0.0).then_inc(prep_step, 1)
                for t in range(T):
                    dve.bn_aggr(mv[:, t, :], stats[:, t, :]).then_inc(prep_step, 1)
                dve.wait_ge(prep_step, at(b, PREP_STEPS, PREP["VAR_IN"]))
                dve.tensor_scalar(vare[:], mv[:, :, 1], LN_EPS, None, ALU.add).then_inc(prep_step, 1)

            def ln_apply(b):
                dve.wait_ge(ln_rstd, at(b, 1, 1))
                for t in range(T):
                    dve.tensor_scalar(xn[:, t, :], xs[b[1]][:, t, :], mv[:, t, 0:1], rstd[:, t:t + 1],
                                                    ALU.subtract, ALU.mult).then_inc(prep_step, 1)

            def xnT_evacuate(b):
                dve.wait_ge(xnT_psum, at(b, 1, 1))
                dve.tensor_copy(xnT[b[1]][:], misc[:, 0:S]).then_inc(misc_evacuated, 1)

            def proj_evacuate(b, turn):
                dve.wait_ge(proj_psum, at(b, 1, 1))
                dve.tensor_copy(proj[:].rearrange("p t n -> p (t n)"), misc[:, 0:T * NPROJ]).then_inc(misc_evacuated, 1)
                dve.wait_ge(misc_evacuated, turn + 2)
                qk = proj[:, :, 0:QKH * HD]
                dve.tensor_tensor(sq[:], qk, qk, ALU.mult).then_inc(prep_step, 1)
                lg = proj[:, :, NPROJ - NE:NPROJ]
                for t in range(T):
                    dve.max(top[:, t, :], lg[:, t, :]).then_inc(prep_step, 1)
                dve.wait_ge(prep_step, at(b, PREP_STEPS, PREP["SQUARES"]))
                dve.tensor_reduce(ms[:], sq[:].rearrange("p t (h e) -> p (t h) e", e=HD), AX.X, ALU.add).then_inc(prep_step, 1)
                for t in range(T):
                    dve.max_index(topi[:, t, :], top[:, t, :], lg[:, t, :]).then_inc(prep_step, 1)
                dve.wait_ge(prep_step, at(b, PREP_STEPS, PREP["SUMS"]))
                dve.tensor_scalar(ms[:], ms[:], 1.0 / HD, RMS_EPS, ALU.mult, ALU.add).then_inc(prep_step, 1)
                dve.tensor_tensor(ldiff[:], top[:, :, 1], top[:, :, 0], ALU.subtract).then_inc(prep_step, 1)
                dve.tensor_copy(topf[:], topi[:, :, 0:2]).then_inc(prep_step, 1)

            def gates(b):
                dve.wait_ge(prep_exp, at(b, 1, 1))
                dve.tensor_scalar(wden[:], eldiff[:], 1.0, None, ALU.add).then_inc(prep_step, 1)
                dve.tensor_scalar(gden[:], egate[:], 1.0, None, ALU.add).then_inc(prep_step, 1)
                dve.wait_ge(prep_step, at(b, PREP_STEPS, PREP["DEN"]))
                dve.reciprocal(wtop[:, 0, :], wden[:]).then_inc(prep_step, 1)
                dve.reciprocal(gsig[:], gden[:]).then_inc(prep_step, 1)
                dve.wait_ge(prep_step, at(b, PREP_STEPS, PREP["WTOP0"]))
                dve.tensor_tensor(wtop[:, 1, :], wtop[:, 0, :], eldiff[:], ALU.mult).then_inc(prep_step, 1)
                for kb in range(2):
                    v = proj[:, kb, D + KV:D + 2 * KV].rearrange("p (g f d) -> p g f d", g=KVH, f=2)
                    s = gsig[:, kb, :].rearrange("p (g f d) -> p g f d", g=KVH, f=2)
                    dve.tensor_tensor(vw_view(b[1], kb, 0, HALF), v, s, ALU.mult).then_inc(v_ready, 1)
                dve.wait_ge(prep_step, at(b, PREP_STEPS, PREP["WTOP1"]))
                for t in range(T):
                    for j, dst in ((0, s0), (1, s1)):
                        dve.tensor_scalar(dst[:, t, :], iota8[:], topf[:, t, j:j + 1], wtop[:, j, t:t + 1],
                                                    ALU.is_equal, ALU.mult).then_inc(prep_step, 1)
                dve.wait_ge(prep_step, at(b, PREP_STEPS, PREP["ONEHOT"]))
                dve.tensor_tensor(score[b[1]][:], s0[:], s1[:], ALU.add).then_inc(prep_step, 1)

            def sT_evacuate(b):
                dve.wait_ge(sT_psum, at(b, 1, 1))
                dve.tensor_copy(scoreT[b[1]][:], misc[0:NE, 0:S]).then_inc(misc_evacuated, 1)

            def rotate_a(b):
                dve.wait_ge(rms_inv, at(b, 1, 1))
                dve.tensor_tensor(rg[:], rinv[:], qmul[:].rearrange("p t h -> p (t h)"), ALU.mult).then_inc(prep_step, 1)
                dve.wait_ge(prep_step, at(b, PREP_STEPS, PREP["RG"]))
                qk = proj[:, :, 0:QKH * HD].rearrange("p t (h e) -> p t h e", e=HD)
                rgb = rg[:].rearrange("p (t h) -> p t h", t=T).unsqueeze(3).to_broadcast([P, T, QKH, HD])
                dve.tensor_tensor(xr[:], qk, rgb, ALU.mult).then_inc(prep_step, 1)
                dve.wait_ge(prep_step, at(b, PREP_STEPS, PREP["XR"]))
                cosb = cos_sb[:].unsqueeze(2).to_broadcast([P, T, QKH, HD])
                dve.tensor_tensor(ra[:], xr[:], cosb, ALU.mult).then_inc(prep_step, 1)
                for f in range(2):
                    sinb = sin_sb[:, :, f * HALF:(f + 1) * HALF].unsqueeze(2).to_broadcast([P, T, QKH, HALF])
                    dve.tensor_tensor(rb[:, :, :, f * HALF:(f + 1) * HALF],
                                                xr[:, :, :, (1 - f) * HALF:(2 - f) * HALF], sinb, ALU.mult).then_inc(prep_step, 1)
                dve.wait_ge(prep_step, at(b, PREP_STEPS, PREP["ROT"]))
                for t in range(T):
                    def heads(a):
                        return a[:, t, 0:H, :].rearrange("p (g r) e -> p g r e", g=KVH)
                    dve.tensor_tensor(qf[:, t].rearrange("p r g e -> p g r e"), heads(ra), heads(rb), ALU.add).then_inc(prep_step, 1)
                dve.tensor_tensor(kf[:], ra[:, :, H:QKH, :], rb[:, :, H:QKH, :], ALU.add).then_inc(prep_step, 1)

            def split_parts(b):
                dve.wait_ge(prep_step, at(b, PREP_STEPS, PREP["QKF"]))
                n = T * REP * GF
                q4 = qf[:].rearrange("p t r g (f d) -> p (t r g f) d", f=2).unsqueeze(2).to_broadcast([P, n, 2, HALF])
                qv = qp[:].rearrange("p t r a s d -> p (t r a) s d")
                dve.tensor_copy(qv[:, :, 0:2, :], q4).then_inc(prep_step, 1)
                k4 = kf[:].rearrange("p t g (f d) -> p (t g f) d", f=2).unsqueeze(2).to_broadcast([P, T * GF, 2, HALF])
                kv = kp[:].rearrange("p t a (s z) d -> p (t a) s z d", s=2)
                kh, kl = kv[:, :, :, 0, :], kv[:, :, :, 1, :]
                dve.tensor_copy(kh, k4).then_inc(prep_step, 1)
                dve.wait_ge(prep_step, at(b, PREP_STEPS, PREP["HIGH"]))
                dve.tensor_tensor(qv[:, :, 2:4, :], q4, qv[:, :, 0:2, :], ALU.subtract).then_inc(prep_step, 1)
                dve.tensor_tensor(kl, k4, kh, ALU.subtract).then_inc(prep_step, 1)

            def qT_evacuate(b):
                dve.wait_ge(qT_psum, at(b, 1, 1))
                dve.tensor_copy(qT[b[1]][:].rearrange("p r s -> p (r s)"), misc16[:, 0:REP * S]).then_inc(misc_evacuated, 1)

            def kT_evacuate(b, turn):
                dve.wait_ge(kT_psum, at(b, 1, 1))
                dve.tensor_copy(kT[:], misc16[:, 0:S]).then_inc(misc_evacuated, 1)
                dve.wait_ge(misc_evacuated, turn + 2)
                for gf in range(GF):
                    dve.tensor_scalar(kpad[b[1]][:, gf, :], kT[:], gfm_sb[:, gf:gf + 1], None, ALU.mult)\
                       .then_inc(k_ready, 1)

            def exact_maxima(b):
                with dve.If(general_path):
                    for n in range(ROUNDS):
                        dve.wait_ge(max_psum, at(b, ROUNDS + 1, n + 1))
                        t, gfs = (0, (2 * n, 2 * n + 1)) if n < 4 else (1, (n - 4,))
                        m = len(gfs) * REP
                        o = gfs[0] * REP
                        dve.tensor_reduce(nmax[:, t, o:o + m], sbank[0][:].rearrange("p (m w) -> p m w", m=m),
                                          AX.X, ALU.max, negate=True).then_inc(max_read, 1)
                    dve.wait_ge(max_psum, at(b, ROUNDS + 1, ROUNDS + 1))
                    dve.tensor_copy(nmaxT[:], sbank[0][0:32, 0:S]).then_inc(max_read, 1)

            def pv_evacuate(b):
                dve.wait_ge(pv_done, at(b, UNITS, UNITS + RING))
                dve.tensor_copy(pvs[:], pvbank[:]).then_inc(pv_evacuated, 1)

            def normalise(b):
                dve.wait_ge(pvT_psum, at(b, 1, 1))
                v = misc[:].rearrange("p (n e) -> p n e", e=8)
                dve.reciprocal(pinv[:], v[:, :, HALF]).then_inc(tail_step, 1)
                dve.wait_ge(tail_step, at(b, TAIL_STEPS, 1))
                dve.tensor_tensor(an[:].rearrange("p t (n d) -> p (t n) d", d=HALF), v[:, :, 0:HALF],
                                  pinv[:].unsqueeze(2).to_broadcast([P, 64, HALF]), ALU.mult).then_inc(misc_evacuated, 1)

            def aT_evacuate(b):
                dve.wait_ge(aT_psum, at(b, 1, 1))
                dve.tensor_copy(aT[:], misc[:, 0:S]).then_inc(misc_evacuated, 1)

            def final_add(b, turn):
                dve.wait_ge(attn_psum, at(b, 1, 1))
                dve.wait_ge(comb_done, at(b, NE, NE + 1))
                dve.wait_ge(out_stored[b[1]], 16 * b[0] + 16)
                dve.tensor_tensor(ofin[b[1]][:].rearrange("p t d -> p (t d)"), misc[:, 0:S],
                                  acc[b[1]][:].rearrange("p t d -> p (t d)"), ALU.add).then_inc(misc_evacuated, 1)

            def combine(b, e):
                dve.wait_ge(y_psum, at(b, NE, e + 3))
                dve.wait_ge(comb_done, at(b, NE, e + 1))
                for t in range(T):
                    prior = xs[b[1]] if e == 0 else acc[b[1]]
                    last = dve.scalar_tensor_tensor(out=acc[b[1]][:, t, :], in0=ybank[:, t * P:(t + 1) * P],
                                                    scalar=score[b[1]][:, t, e:e + 1], in1=prior[:, t, :],
                                                    op0=ALU.mult, op1=ALU.add)
                last.then_inc(comb_done, 1)

            def seq(b, nxt, prv):
                for k in range(UNITS):
                    if 2 <= k < NE + 2:
                        combine(b, k - 2)
                    if k == 0:
                        if prv is not None:
                            pv_evacuate(prv)
                        if nxt is not None:
                            ln_stats(nxt)
                        if prv is not None:
                            normalise(prv)
                        if nxt is not None:
                            ln_apply(nxt)
                    if k == 1 and prv is not None:
                        aT_evacuate(prv)
                    if k == 2 and prv is not None:
                        final_add(prv, misc_turn(b, TAIL_OUT))
                    if nxt is None:
                        continue
                    if k == PREP_XNT:
                        xnT_evacuate(nxt)
                    if k == PREP_PROJ:
                        proj_evacuate(nxt, misc_turn(b, PREP_PROJ))
                    if k == 6:
                        gates(nxt)
                    if k == 7:
                        rotate_a(nxt)
                        sT_evacuate(nxt)
                    if k == 8:
                        split_parts(nxt)
                    if k == PREP_QT:
                        qT_evacuate(nxt)
                    if k == PREP_KT:
                        kT_evacuate(nxt, misc_turn(b, PREP_KT))
                if nxt is not None:
                    exact_maxima(nxt)

            general_path = dve.value_load(big_i[0:1, 0:1], min_val=0, max_val=1)
            first = (0, 0)
            ln_stats(first)
            ln_apply(first)
            xnT_evacuate(first)
            proj_evacuate(first, misc_turn(None, PREP_PROJ))
            gates(first)
            sT_evacuate(first)
            rotate_a(first)
            split_parts(first)
            qT_evacuate(first)
            kT_evacuate(first, misc_turn(None, PREP_KT))
            exact_maxima(first)
            last = schedule(dve, seq)
            pv_evacuate(last)
            normalise(last)
            aT_evacuate(last)
            final_add(last, misc_turn(last, TAIL_OUT, past=True))


def tables():
    pos = np.arange(S, dtype=np.float32)
    angles = np.arange(0, HD, 2, dtype=np.float32) / np.float32(HD) * np.float32(math.pi)
    radius = np.float32(1.0) / (np.float32(1.0) + pos[:, None] * np.float32(0.01))
    ang = pos[:, None] * angles[None, :]
    cos, sin = radius * np.cos(ang), radius * np.sin(ang)
    cos_t = np.concatenate([cos, cos], 1).reshape(T, P, HD).transpose(1, 0, 2)
    sin_t = np.concatenate([sin, -sin], 1).reshape(T, P, HD).transpose(1, 0, 2)
    gf_mask = (np.arange(P)[:, None] // 16 == np.arange(GF)[None, :]).astype(np.float32)
    ident = np.eye(P, dtype=np.float32)
    causal = np.where(np.arange(P)[None, :] > np.arange(P)[:, None], NEG, 0.0).astype(np.float32)
    return cos_t, sin_t, gf_mask, ident, causal


def kernel(L0_attn_x, L0_attn_Wq, L0_attn_Wk, L0_attn_Wv, L0_attn_Wg, L0_attn_Wo, L0_attn_q_gain,
           L0_attn_lambda_param, L0_ffn_Wg, L0_ffn_W1, L0_ffn_b1, L0_ffn_W2, L0_ffn_b2):
    import concourse.bacc as _bacc
    from concourse.bass_utils import run_bass_kernel_spmd as _run

    a = np.asarray
    cos_t, sin_t, gf_mask, ident, causal = tables()
    w_proj = np.concatenate([a(L0_attn_Wq).T, a(L0_attn_Wk).T, a(L0_attn_Wv).T, a(L0_attn_Wg).T, a(L0_ffn_Wg)], axis=1)
    wo = a(L0_attn_Wo).T.reshape(KVH, REP, 2, HALF, D).transpose(2, 1, 0, 3, 4).reshape(2, D // 2, D)
    lam = np.repeat(a(L0_attn_lambda_param).reshape(KVH, REP).T.reshape(H), HALF)[:, None]
    arrays = {
        "x": a(L0_attn_x),
        "w_proj": w_proj,
        "wo_a": np.concatenate([wo[0], wo[0]]),
        "wo_b": np.concatenate([wo[1], wo[1]]),
        "gain": np.broadcast_to(a(L0_attn_q_gain)[None, :], (P, H)),
        "lam_col": np.concatenate([np.ones((D // 2, 1), np.float32), lam]),
        "w1": a(L0_ffn_W1).transpose(1, 0, 2),
        "b1": a(L0_ffn_b1).reshape(NE, HC, P).transpose(2, 0, 1),
        "w2": a(L0_ffn_W2).reshape(NE, HC, P, D).transpose(2, 0, 1, 3),
        "b2": a(L0_ffn_b2),
        "cos_t": cos_t,
        "sin_t": sin_t,
        "gf_mask": gf_mask,
        "ident": ident,
        "causal_neg": causal,
    }
    arrays = {n: np.ascontiguousarray(v) for n, v in arrays.items()}
    nc = _bacc.Bacc("TRN2", target_bir_lowering=False, num_devices=1)
    args = {n: nc.dram_tensor(f"in_{n}", v.shape, mybir.dt.from_np(v.dtype), kind="ExternalInput").ap()
            for n, v in arrays.items()}
    out = nc.dram_tensor("out_y", (NB, S, D), F32, kind="ExternalOutput").ap()
    moe_attention_kernel(nc, out=out, **args)
    r = _run(nc, [{f"in_{n}": v for n, v in arrays.items()}], core_ids=[0])
    return r.results[0]["out_y"]
```

```python
import math
from contextlib import ExitStack

import numpy as np

import concourse.bass as bass
from concourse import mybir

F32 = mybir.dt.float32
F16 = mybir.dt.float16
BF16 = mybir.dt.bfloat16
I32 = mybir.dt.int32
U32 = mybir.dt.uint32
ALU = mybir.AluOpType
ACT = mybir.ActivationFunctionType
AX = mybir.AxisListType

P = 128
NB, S, D = 32, 256, 128
T = S // P
H, KVH = 16, 4
HD = D // H
HALF = HD // 2
REP = H // KVH
KV = KVH * HD
GF = KVH * 2
NE, HID = 8, 256
HC = HID // P
NPROJ = D + 3 * KV + NE
QKH = H + KVH
UNITS = 12
UW = 1024
RING = 4
LN_EPS = 1e-5
RMS_EPS = float(np.finfo(np.float32).eps)
SCALE = 1.0 / math.sqrt(HALF)
RSQRT_MAGIC = 0x5F3759DF
GAIN_LIMIT = 8.0
NEG = -3.0e38

NEWTON = 3 * 3
_stages = {
    "STATS": T, "VAR_IN": 1 + T, "VAR": 1, "LN_GUESS": 3, "LN_RSTD": NEWTON, "XN": T,
    "SQUARES": 1 + T, "SUMS": 1 + T, "MS": 1, "LDIFF": 1, "TOPF": 1, "RMS_GUESS": 3, "RMS_INV": NEWTON,
    "RG": 1, "XR": 1, "ROT": 3, "KF": 1, "K_HIGH": 1, "KP": 1, "QF": T, "Q_HIGH": 1, "QP": 1,
    "DEN": 2, "WTOP0": 2, "WTOP1": 1, "ONEHOT": 2 * T, "SCORE": 1,
}
PREP = dict(zip(_stages, (int(n) for n in np.cumsum(list(_stages.values())))))
PREP_STEPS = PREP["SCORE"]
TAIL_STEPS = 1
SETUP_STEPS = 33
WEIGHTS = 14 * 16

UNIT = []
for _f in range(2):
    for _pair in range(KVH // 2):
        _g = 2 * _pair
        UNIT += [(_f, 0, (_g,)), (_f, 0, (_g + 1,)), (_f, 1, (_g, _g + 1))]
assert len(UNIT) == UNITS

TAIL_SLOTS = {"pv_t": 0, "a_t": 1, "attn_out": 3}
PREP_SLOTS = {"xn_t": 2, "proj": 4, "k_t": 8, "q_t": 9, "score_t": 10}
EXPERT_IN_SLOTS = [0, 1, 2, 4, 5, 6, 8, 9]
EXPERT_OUT_SLOTS = [1, 3, 4, 6, 7, 8, 10, 11]
MISC_ORDER = ["pv_t", "a_t", "xn_t", "attn_out", "proj", "k_t", "q_t", "score_t"]
ROUNDS = 12


LAST = (NB // 2 - 1, 1)


def at(b, per, k):
    return (2 * per) * b[0] + (per * b[1] + k)


def after(b):
    return b[0] + b[1], 1 - b[1]


def before(b):
    return b[0] - (1 - b[1]), 1 - b[1]


def moe_attention_kernel(nc, x, w_proj, wo_a, wo_b, gain, lam_col, w1, b1, w2, b2, cos_t, sin_t, gf_mask, ident, causal_neg, out):
    ctx = ExitStack()
    with ctx:
        def sb(name, shape, dt=F32):
            return ctx.enter_context(nc.sbuf_tensor(name, shape, dt))

        def pb(name, shape, dt=F32):
            return ctx.enter_context(nc.psum_tensor(name, shape, dt))

        def sem(name):
            return ctx.enter_context(nc.semaphore(name))

        wproj_sb = sb("wproj_sb", [P, NPROJ])
        woa_sb = sb("woa_sb", [P, D])
        wob_sb = sb("wob_sb", [P, D])
        wo_sb = sb("wo_sb", [P, D])
        lamc = sb("lamc", [P, 1])
        lamn = sb("lamn", [P, 1])
        w1_sb = sb("w1_sb", [P, NE, HID])
        b1_sb = sb("b1_sb", [P, NE, HC])
        w2_sb = sb("w2_sb", [P, NE, HC, D])
        b2_sb = sb("b2_sb", [NE, D])
        cos_sb = sb("cos_sb", [P, T, HD])
        sin_sb = sb("sin_sb", [P, T, HD])
        gfm_sb = sb("gfm_sb", [P, GF])
        id32 = sb("id32", [P, P])
        id16 = sb("id16", [P, P], F16)
        idb = sb("idb", [P, P], BF16)
        neg32 = sb("neg32", [P, P])
        negb = sb("negb", [P, P], BF16)
        gain_sb = sb("gain_sb", [P, H])
        gabs = sb("gabs", [P, H])
        gmax = sb("gmax", [P, 1])
        big = sb("big", [P, 1])
        big_i = sb("big_i", [P, 1], I32)
        gsgn = sb("gsgn", [P, H])
        gtmp = sb("gtmp", [P, H])
        qmul = sb("qmul", [P, T, QKH])
        iota8 = sb("iota8", [P, NE])
        rt0 = sb("rt0", [P, T * QKH])
        rt1 = sb("rt1", [P, T * QKH])

        xs = [sb(f"xs{i}", [P, T, D]) for i in range(2)]
        stats = sb("stats", [P, T, 6])
        mv = sb("mv", [P, T, 2])
        vare = sb("vare", [P, T])
        rstd = sb("rstd", [P, T])
        xn = sb("xn", [P, T, D])
        xnT = [sb(f"xnT{i}", [P, S]) for i in range(2)]
        proj = sb("proj", [P, T, NPROJ])
        sq = sb("sq", [P, T, QKH * HD])
        ms = sb("ms", [P, T * QKH])
        rinv = sb("rinv", [P, T * QKH])
        rg = sb("rg", [P, T * QKH])
        xr = sb("xr", [P, T, QKH, HD])
        ra = sb("ra", [P, T, QKH, HD])
        rb = sb("rb", [P, T, QKH, HD])
        qf = sb("qf", [P, T, REP, KVH, HD])
        kf = sb("kf", [P, T, KVH, HD])
        qp = sb("qp", [P, T, REP, GF, 4, HALF], F16)
        kp = sb("kp", [P, T, GF, 4, HALF], F16)
        qT = [sb(f"qT{i}", [P, REP, S], F16) for i in range(2)]
        kT = sb("kT", [P, S], F16)
        kpad = [sb(f"kpad{i}", [P, GF, S], F16) for i in range(2)]
        egate = sb("egate", [P, T, KV])
        gden = sb("gden", [P, T, KV])
        gsig = sb("gsig", [P, T, KV])
        vw = [sb(f"vw{i}", [P, 2 * GF * 32 + 32]) for i in range(2)]
        top = sb("top", [P, T, 8])
        topi = sb("topi", [P, T, 8], U32)
        topf = sb("topf", [P, T, 2])
        ldiff = sb("ldiff", [P, T])
        eldiff = sb("eldiff", [P, T])
        wden = sb("wden", [P, T])
        wtop = sb("wtop", [P, 2, T])
        s0 = sb("s0", [P, T, NE])
        s1 = sb("s1", [P, T, NE])
        score = [sb(f"score{i}", [P, T, NE]) for i in range(2)]
        scoreT = [sb(f"scoreT{i}", [NE, S]) for i in range(2)]
        probs = [sb(f"probs{i}", [P, UW]) for i in range(RING)]
        hT = [sb(f"hT{i}", [P, HC, S]) for i in range(2)]
        acc = [sb(f"acc{i}", [P, T, D]) for i in range(2)]
        pvs = sb("pvs", [P, 2, S])
        pinv = sb("pinv", [P, 64])
        an = sb("an", [P, T, D])
        aT = sb("aT", [P, S])
        ofin = [sb(f"ofin{i}", [P, T, D]) for i in range(2)]
        nmax = sb("nmax", [P, T, 32])
        nmaxT = sb("nmaxT", [32, S])
        credits = sb("credits", [P, 16])
        hold = sb("hold", [P, 1])

        sbank = [pb(f"sbank{i}", [P, UW]) for i in range(2)]
        pvbank = pb("pvbank", [P, 2, S])
        hbank = pb("hbank", [P, HC, S])
        ybank = pb("ybank", [P, 512])
        misc = pb("misc", [P, 512])
        misc16 = misc[:, :].bitcast(F16)

        def vw_view(p, kb, c0, c1):
            flat = vw[p][:, kb * 256:kb * 256 + 288].rearrange("p (g x) -> p g x", g=KVH)
            return flat[:, :, 0:64].rearrange("p g (f y) -> p g f y", f=2)[:, :, :, c0:c1]

        weights_in = sem("weights_in")
        x_in = [sem(f"x_in{i}") for i in range(2)]
        out_stored = [sem(f"out_stored{i}") for i in range(2)]
        setup = sem("setup")
        prep_step = sem("prep_step")
        tail_step = sem("tail_step")
        prep_exp = sem("prep_exp")
        v_ready = sem("v_ready")
        k_ready = sem("k_ready")
        xnT_psum = sem("xnT_psum")
        proj_psum = sem("proj_psum")
        sT_psum = sem("sT_psum")
        qT_psum = sem("qT_psum")
        kT_psum = sem("kT_psum")
        pvT_psum = sem("pvT_psum")
        aT_psum = sem("aT_psum")
        attn_psum = sem("attn_psum")
        misc_evacuated = sem("misc_evacuated")
        scores_ready = sem("scores_ready")
        exp_done = [sem(f"exp_done{i}") for i in range(RING)]
        mask_done = sem("mask_done")
        pv_done = sem("pv_done")
        pv_evacuated = sem("pv_evacuated")
        h_psum = sem("h_psum")
        relu_done = sem("relu_done")
        y_psum = sem("y_psum")
        comb_done = sem("comb_done")
        max_psum = sem("max_psum")
        max_read = sem("max_read")

        block = ctx.enter_context(nc.Block())

        def misc_turn(step, b, tail, prep, past=False):
            kinds = [k for k in MISC_ORDER if (k in TAIL_SLOTS and tail) or (k in PREP_SLOTS and prep)]
            n = kinds.index(step)
            if b is None:
                return n
            if not tail:
                return len(PREP_SLOTS) + n
            return at(b, len(MISC_ORDER), 2 * len(PREP_SLOTS) - len(MISC_ORDER) + n + (len(TAIL_SLOTS) if past else 0))

        def schedule(eng, seq):
            a, z = (0, 0), (0, 1)
            seq(a, z, None)
            seq(z, after(z), a)
            with eng.Fori(1, NB // 2 - 1) as i:
                for p in range(2):
                    b = (i, p)
                    seq(b, after(b), before(b))
            a, z = (NB // 2 - 1, 0), (NB // 2 - 1, 1)
            seq(a, z, before(a))
            seq(z, None, a)

        @block.sync
        def _(sp):
            xr_ = x.rearrange("b (t p) d -> b p t d", p=P)
            or_ = out.rearrange("b (t p) d -> b p t d", p=P)
            sp.dma_start(xs[0][:], xr_[0]).then_inc(x_in[0], 16)
            for dst, src in ((wproj_sb[:], w_proj), (id32[:], ident), (gain_sb[:], gain), (cos_sb[:], cos_t),
                             (sin_sb[:], sin_t), (gfm_sb[:], gf_mask), (neg32[:], causal_neg),
                             (woa_sb[:], wo_a), (wob_sb[:], wo_b), (lamc[:], lam_col), (b1_sb[:], b1),
                             (b2_sb[:], b2), (w1_sb[:], w1), (w2_sb[:], w2)):
                sp.dma_start(dst, src).then_inc(weights_in, 16)
            sp.dma_start(xs[1][:], xr_[1]).then_inc(x_in[1], 16)

            def store(b, turn):
                sp.wait_ge(misc_evacuated, turn + 2)
                sp.dma_start(or_[2 * b[0] + b[1]], ofin[b[1]][:]).then_inc(out_stored[b[1]], 16)

            def seq(b, nxt, prv):
                if prv is not None:
                    store(prv, misc_turn("attn_out", b, True, nxt is not None))
                if not (isinstance(b[0], int) and b[0] == NB // 2 - 1):
                    sp.wait_ge(comb_done, at(b, NE, 2))
                    sp.dma_start(xs[b[1]][:], xr_[2 * b[0] + (b[1] + 2)]).then_inc(x_in[b[1]], 16)

            schedule(sp, seq)
            store(LAST, misc_turn("attn_out", LAST, True, False, past=True))
            for p in range(2):
                sp.wait_ge(out_stored[p], 16 * (NB // 2 + 1))

        @block.tensor
        def _(pe):
            def xn_transposes(b, turn):
                pe.wait_ge(misc_evacuated, turn + 1)
                pe.wait_ge(prep_step, at(b, PREP_STEPS, PREP["XN"]))
                for t in range(T):
                    last = pe.transpose(misc[:, t * P:(t + 1) * P], xn[:, t, :], id32[:])
                last.then_inc(xnT_psum, 1)

            def projection(b, turn):
                pe.wait_ge(misc_evacuated, turn + 1)
                for t in range(T):
                    last = pe.matmul(misc[:, t * NPROJ:(t + 1) * NPROJ], xnT[b[1]][:, t * P:(t + 1) * P],
                                     wproj_sb[:], start=True, stop=True)
                last.then_inc(proj_psum, 1)

            def score_transposes(b, turn):
                pe.wait_ge(misc_evacuated, turn + 1)
                pe.wait_ge(prep_step, at(b, PREP_STEPS, PREP["SCORE"]))
                for t in range(T):
                    last = pe.transpose(misc[0:NE, t * P:(t + 1) * P], score[b[1]][:, t, :], id32[:])
                last.then_inc(sT_psum, 1)

            def q_transposes(b, turn):
                pe.wait_ge(misc_evacuated, turn + 1)
                pe.wait_ge(prep_step, at(b, PREP_STEPS, PREP["QP"]))
                for r in range(REP):
                    for t in range(T):
                        o = (r * T + t) * P
                        last = pe.transpose(misc16[:, o:o + P], qp[:, t, r].rearrange("p a b c -> p (a b c)"), id16[:])
                last.then_inc(qT_psum, 1)

            def k_transposes(b, turn):
                pe.wait_ge(misc_evacuated, turn + 1)
                pe.wait_ge(prep_step, at(b, PREP_STEPS, PREP["KP"]))
                for t in range(T):
                    last = pe.transpose(misc16[:, t * P:(t + 1) * P], kp[:, t].rearrange("p a b c -> p (a b c)"), id16[:])
                last.then_inc(kT_psum, 1)

            def pv_transposes(b, turn):
                pe.wait_ge(misc_evacuated, turn + 1)
                pe.wait_ge(pv_evacuated, at(b, 1, 2))
                for t in range(T):
                    for f in range(2):
                        o = (t * 2 + f) * P
                        last = pe.transpose(misc[:, o:o + P], pvs[:, f, t * P:(t + 1) * P], id32[:])
                last.then_inc(pvT_psum, 1)

            def a_transposes(b, turn):
                pe.wait_ge(misc_evacuated, turn + 1)
                for t in range(T):
                    last = pe.transpose(misc[:, t * P:(t + 1) * P], an[:, t, :], id32[:])
                last.then_inc(aT_psum, 1)

            def attention_out(b, turn):
                pe.wait_ge(misc_evacuated, turn + 1)
                for t in range(T):
                    o = misc[:, t * P:(t + 1) * P]
                    pe.matmul(o, aT[:, t * P:(t + 1) * P], wo_sb[:], start=True, stop=False)
                    last = pe.matmul(o, scoreT[b[1]][:, t * P:(t + 1) * P], b2_sb[:], start=False, stop=True)
                last.then_inc(attn_psum, 1)

            def score_unit(b, u, general):
                f, kb, gs = UNIT[u]
                bank = sbank[u % 2]
                for n in range(2):
                    if kb == 0:
                        rhs, g = qT[b[1]][:, 2 * n:2 * n + 2, :], gs[0]
                    else:
                        rhs, g = qT[b[1]][:, :, P:S], gs[n]
                    gf = 2 * g + f
                    o = bank[:, n * 512:(n + 1) * 512]
                    last = pe.matmul(o, kpad[b[1]][:, gf, kb * P:(kb + 1) * P], rhs, start=True, stop=not general,
                                     skip_group_check=general)
                    if general:
                        heads = (2 * n, 2 * n + 1) if kb == 0 else range(REP)
                        w = S // (kb + 1)
                        for j, r in enumerate(heads):
                            hh = gf * REP + r
                            last = pe.matmul(o[:, j * w:(j + 1) * w], id32[0:32, hh:hh + 1].to_broadcast([32, P]),
                                             nmaxT[:, kb * P:S], start=False, stop=True, skip_group_check=True)
                last.then_inc(scores_ready, 1)

            def scores(b, u, general, turn=None):
                pe.wait_ge(mask_done, at(b, UNITS, u + 1))
                if turn is not None:
                    pe.wait_ge(misc_evacuated, turn + 2)
                    pe.wait_ge(k_ready, at(b, GF, GF))
                score_unit(b, u, general)

            def exact_maxima(b, current, turn):
                pe.wait_ge(misc_evacuated, turn + 2)
                pe.wait_ge(k_ready, at(b, GF, GF))
                if current is not None:
                    pe.wait_ge(mask_done, at(current, UNITS, UNITS + 1))
                for n in range(ROUNDS):
                    pe.wait_ge(max_read, at(b, ROUNDS + 1, n + 1))
                    t, gfs = (0, (2 * n, 2 * n + 1)) if n < 4 else (1, (n - 4,))
                    w = (t + 1) * P
                    for j, gf in enumerate(gfs):
                        for r in range(REP):
                            o = sbank[0][:, (j * REP + r) * w:(j * REP + r + 1) * w]
                            pe.matmul(o, qT[b[1]][:, r, t * P:(t + 1) * P], kpad[b[1]][:, gf, 0:w],
                                      start=True, stop=False, skip_group_check=True)
                            last = pe.matmul(o[:, t * P:w], idb[:], negb[:], start=False, stop=True,
                                             skip_group_check=True)
                    last.then_inc(max_psum, 1)
                pe.wait_ge(max_read, at(b, ROUNDS + 1, ROUNDS + 1))
                for t in range(T):
                    last = pe.transpose(sbank[0][0:32, t * P:(t + 1) * P], nmax[:, t, :], id32[:])
                last.then_inc(max_psum, 1)
                pe.wait_ge(max_read, at(b, ROUNDS + 1, ROUNDS + 2))

            def values(b, u):
                f, kb, gs = UNIT[u]
                pe.wait_ge(mask_done, at(b, UNITS, u + 3))
                if u == 0:
                    pe.wait_ge(v_ready, at(b, 2, 2))
                    pe.wait_ge(pv_evacuated, at(b, 1, 1))
                for n, g in enumerate(gs):
                    gf = 2 * g + f
                    for r in range(REP):
                        w = S // (kb + 1)
                        rhs = probs[u % RING][:, (n * REP + r) * w:(n * REP + r + 1) * w]
                        last = pe.matmul(pvbank[32 * r:32 * r + 32, f, kb * P:S],
                                         vw[b[1]][:, (kb * GF + gf) * 32:(kb * GF + gf + 1) * 32], rhs,
                                         start=(g == 0 and kb == 0), stop=(g == KVH - 1 and kb == 1),
                                         skip_group_check=True)
                last.then_inc(pv_done, 1)

            def expert_in(b, e):
                pe.wait_ge(relu_done, at(b, NE, e + 1))
                for c in range(HC):
                    last = pe.matmul(hbank[:, c, :], w1_sb[:, e, c * P:(c + 1) * P], xnT[b[1]][:],
                                     start=True, stop=True)
                last.then_inc(h_psum, 1)

            def expert_out(b, e):
                pe.wait_ge(relu_done, at(b, NE, e + 2))
                pe.wait_ge(comb_done, at(b, NE, e + 1))
                for t in range(T):
                    for c in range(HC):
                        last = pe.matmul(ybank[:, t * P:(t + 1) * P], hT[e % 2][:, c, t * P:(t + 1) * P],
                                         w2_sb[:, e, c, :], start=(c == 0), stop=(c == HC - 1))
                last.then_inc(y_psum, 1)

            def seq(b, nxt, prv, general):
                for u in range(UNITS):
                    if u < UNITS - 1:
                        scores(b, u + 1, general)
                    elif nxt is not None:
                        turn = misc_turn("q_t", b, prv is not None, True)
                        if general:
                            exact_maxima(nxt, b, turn)
                        scores(nxt, 0, general, turn)
                    if u in EXPERT_OUT_SLOTS:
                        expert_out(b, EXPERT_OUT_SLOTS.index(u))
                    if u in EXPERT_IN_SLOTS:
                        expert_in(b, EXPERT_IN_SLOTS.index(u))
                    for name, step in tail_steps.items():
                        if prv is not None and u == TAIL_SLOTS[name]:
                            step(prv, misc_turn(name, b, True, nxt is not None))
                    for name, step in prep_steps.items():
                        if nxt is not None and u == PREP_SLOTS[name]:
                            step(nxt, misc_turn(name, b, prv is not None, True))
                    values(b, u)

            prep_steps = {"xn_t": xn_transposes, "proj": projection, "k_t": k_transposes, "q_t": q_transposes,
                          "score_t": score_transposes}
            tail_steps = {"pv_t": pv_transposes, "a_t": a_transposes, "attn_out": attention_out}
            pe.wait_ge(weights_in, WEIGHTS)
            pe.wait_ge(setup, SETUP_STEPS)
            general_path = pe.value_load(big_i[0:1, 0:1], min_val=0, max_val=1)
            for name, step in prep_steps.items():
                step((0, 0), misc_turn(name, None, False, True))

            def all_sequences(general):
                turn = misc_turn("q_t", None, False, True)
                if general:
                    exact_maxima((0, 0), None, turn)
                scores((0, 0), 0, general, turn)
                schedule(pe, lambda b, nxt, prv: seq(b, nxt, prv, general))

            with pe.If(general_path):
                all_sequences(True)
            with pe.Else():
                all_sequences(False)
            for name, step in tail_steps.items():
                step(LAST, misc_turn(name, LAST, True, False, past=True))

        @block.scalar
        def _(act):
            def exps(b, u, general):
                act.wait_ge(pv_done, at(b, UNITS, u + 1))
                act.wait_ge(scores_ready, at(b, UNITS, u + 1))
                f, kb, gs = UNIT[u]
                dst, src = probs[u % RING], sbank[u % 2]
                if general:
                    w = S // (kb + 1)
                    for n, g in enumerate(gs):
                        for r in range(REP):
                            a, h = (n * REP + r) * w, g * REP + r
                            last = nc.scalar.activation(dst[:, a:a + w], src[:, a:a + w], ACT.Exp,
                                                        scale=gabs[:, h:h + 1])
                    last.then_inc(exp_done[u % RING], 1)
                else:
                    nc.scalar.activation(dst[:], src[:], ACT.Exp).then_inc(exp_done[u % RING], 1)

            def relus(b, e):
                act.wait_ge(h_psum, at(b, NE, e + 1))
                act.wait_ge(y_psum, at(b, NE, e + 1))
                for c in range(HC):
                    last = nc.scalar.activation(hT[e % 2][:, c, :], hbank[:, c, :], ACT.Relu,
                                                bias=b1_sb[:, e, c:c + 1])
                last.then_inc(relu_done, 1)

            def prep_exps(b):
                act.wait_ge(prep_step, at(b, PREP_STEPS, PREP["LDIFF"]))
                nc.scalar.activation(egate[:], proj[:, :, D + 2 * KV:D + 3 * KV], ACT.Exp, scale=-1.0)
                nc.scalar.activation(eldiff[:], ldiff[:], ACT.Exp).then_inc(prep_exp, 1)

            def seq(b, nxt, prv, general):
                for u in range(UNITS):
                    exps(b, u, general)
                    if u in EXPERT_IN_SLOTS:
                        relus(b, EXPERT_IN_SLOTS.index(u))
                    if u == 6 and nxt is not None:
                        prep_exps(nxt)

            act.wait_ge(weights_in, WEIGHTS)
            act.wait_ge(setup, SETUP_STEPS)
            general_path = act.value_load(big_i[0:1, 0:1], min_val=0, max_val=1)
            prep_exps((0, 0))
            with act.If(general_path):
                schedule(act, lambda b, nxt, prv: seq(b, nxt, prv, True))
            with act.Else():
                schedule(act, lambda b, nxt, prv: seq(b, nxt, prv, False))

        @block.gpsimd
        def _(pool):
            def masks(b, u):
                f, kb, gs = UNIT[u]
                pool.wait_ge(exp_done[u % RING], 1)
                pool.sem_clear(exp_done[u % RING])
                if kb == 0:
                    v = probs[u % RING][:].rearrange("p (r q) -> p r q", r=REP)[:, :, 0:P]
                    n = REP
                else:
                    v = probs[u % RING][:].rearrange("p (r q) -> p r q", r=2 * REP)
                    n = 2 * REP
                nc.gpsimd.affine_select(out=v, in_=v, compare_op=ALU.is_ge, fill=0.0, base=0,
                                        pattern=[[0, n], [1, P]], channel_multiplier=-1).then_inc(mask_done, 1)

            def seq(b, nxt, prv):
                for u in range(UNITS):
                    masks(b, u)

            schedule(pool, seq)

        @block.vector
        def _(dve):
            dve.wait_ge(weights_in, WEIGHTS)
            dve.tensor_copy(id16[:], id32[:]).then_inc(setup, 1)
            dve.tensor_copy(idb[:], id32[:]).then_inc(setup, 1)
            dve.tensor_copy(negb[:], neg32[:]).then_inc(setup, 1)
            for j in range(NE):
                dve.memset(iota8[:, j:j + 1], float(j)).then_inc(setup, 1)
            for p in range(2):
                dve.memset(vw[p][:], 0.0).then_inc(setup, 1)
            dve.wait_ge(setup, 13)
            for p in range(2):
                for kb in range(2):
                    dve.memset(vw_view(p, kb, HALF, HALF + 1), 1.0).then_inc(setup, 1)
            dve.tensor_scalar(gtmp[:], gain_sb[:], -1.0, None, ALU.mult).then_inc(setup, 1)
            dve.wait_ge(setup, 18)
            dve.tensor_tensor(gabs[:], gtmp[:], gain_sb[:], ALU.max).then_inc(setup, 1)
            dve.wait_ge(setup, 19)
            dve.tensor_reduce(gmax[:], gabs[:], AX.X, ALU.max).then_inc(setup, 1)
            dve.tensor_scalar(gsgn[:], gain_sb[:], 0.0, 2.0, ALU.is_ge, ALU.mult).then_inc(setup, 1)
            dve.wait_ge(setup, 21)
            dve.tensor_scalar(big[:], gmax[:], GAIN_LIMIT, None, ALU.is_gt).then_inc(setup, 1)
            dve.scalar_tensor_tensor(out=gtmp[:], in0=gsgn[:], scalar=-1.0, in1=gain_sb[:], op0=ALU.add, op1=ALU.subtract).then_inc(setup, 1)
            dve.wait_ge(setup, 23)
            dve.tensor_copy(big_i[:], big[:]).then_inc(setup, 1)
            dve.scalar_tensor_tensor(out=gsgn[:], in0=gtmp[:], scalar=big[:, 0:1], in1=gain_sb[:], op0=ALU.mult, op1=ALU.add).then_inc(setup, 1)
            dve.wait_ge(setup, 25)
            for t in range(T):
                dve.tensor_scalar(qmul[:, t, 0:H], gsgn[:], SCALE, None, ALU.mult).then_inc(setup, 1)
                dve.memset(qmul[:, t, H:QKH], 1.0).then_inc(setup, 1)
            dve.tensor_scalar(lamn[0:64, :], lamc[0:64, :], 1.0, None, ALU.mult).then_inc(setup, 1)
            dve.tensor_scalar(lamn[64:P, :], lamc[64:P, :], -1.0, None, ALU.mult).then_inc(setup, 1)
            dve.wait_ge(setup, 31)
            dve.tensor_scalar(wo_sb[:], woa_sb[:], lamn[:, 0:1], None, ALU.mult).then_inc(setup, 1)
            dve.wait_ge(setup, 32)
            dve.scalar_tensor_tensor(out=wo_sb[:], in0=wob_sb[:], scalar=lamc[:, 0:1], in1=wo_sb[:], op0=ALU.mult, op1=ALU.add).then_inc(setup, 1)
            dve.wait_ge(setup, SETUP_STEPS)
            n_credit = 0
            for s, v in ((misc_evacuated, 1), (mask_done, 2), (pv_done, RING), (pv_evacuated, 1), (relu_done, 1),
                         (y_psum, 2), (comb_done, 1), (max_read, 1), (out_stored[0], 16), (out_stored[1], 16)):
                dve.memset(credits[:, n_credit:n_credit + 1], 0.0).then_inc(s, v)
                n_credit += 1

            def ln_stats(b):
                dve.wait_ge(x_in[b[1]], 16 * b[0] + 16)
                for t in range(T):
                    dve.bn_stats(stats[:, t, :], xs[b[1]][:, t, :]).then_inc(prep_step, 1)
                dve.wait_ge(prep_step, at(b, PREP_STEPS, PREP["STATS"]))
                dve.memset(hold[:], 0.0).then_inc(prep_step, 1)
                for t in range(T):
                    dve.bn_aggr(mv[:, t, :], stats[:, t, :]).then_inc(prep_step, 1)
                dve.wait_ge(prep_step, at(b, PREP_STEPS, PREP["VAR_IN"]))
                dve.tensor_scalar(vare[:], mv[:, :, 1], LN_EPS, None, ALU.add).then_inc(prep_step, 1)

            def rsqrt(b, y, v, t0, t1, base):
                dve.tensor_single_scalar(t0.bitcast(I32), v.bitcast(I32), 1, ALU.arith_shift_right).then_inc(prep_step, 1)
                dve.tensor_scalar(t1, v, -0.5, None, ALU.mult).then_inc(prep_step, 1)
                dve.wait_ge(prep_step, at(b, PREP_STEPS, base + 2))
                dve.tensor_scalar(y.bitcast(I32), t0.bitcast(I32), -1.0, float(RSQRT_MAGIC), ALU.mult, ALU.add)\
                   .then_inc(prep_step, 1)
                for n in range(NEWTON // 3):
                    dve.wait_ge(prep_step, at(b, PREP_STEPS, base + 3 + 3 * n))
                    dve.tensor_tensor(t0, y, y, ALU.mult).then_inc(prep_step, 1)
                    dve.wait_ge(prep_step, at(b, PREP_STEPS, base + 4 + 3 * n))
                    dve.tensor_tensor(t0, t0, t1, ALU.mult).then_inc(prep_step, 1)
                    dve.wait_ge(prep_step, at(b, PREP_STEPS, base + 5 + 3 * n))
                    dve.scalar_tensor_tensor(out=y, in0=t0, scalar=1.5, in1=y, op0=ALU.add, op1=ALU.mult)\
                       .then_inc(prep_step, 1)

            def ln_apply(b):
                dve.wait_ge(prep_step, at(b, PREP_STEPS, PREP["VAR"]))
                rsqrt(b, rstd[:], vare[:], rt0[:, 0:T], rt1[:, 0:T], PREP["VAR"])
                dve.wait_ge(prep_step, at(b, PREP_STEPS, PREP["LN_RSTD"]))
                for t in range(T):
                    dve.tensor_scalar(xn[:, t, :], xs[b[1]][:, t, :], mv[:, t, 0:1], rstd[:, t:t + 1],
                                                    ALU.subtract, ALU.mult).then_inc(prep_step, 1)

            def xnT_evacuate(b):
                dve.wait_ge(xnT_psum, at(b, 1, 1))
                dve.tensor_copy(xnT[b[1]][:], misc[:, 0:S]).then_inc(misc_evacuated, 1)

            def proj_evacuate(b, turn):
                dve.wait_ge(proj_psum, at(b, 1, 1))
                dve.tensor_copy(proj[:].rearrange("p t n -> p (t n)"), misc[:, 0:T * NPROJ]).then_inc(misc_evacuated, 1)
                dve.wait_ge(misc_evacuated, turn + 2)
                qk = proj[:, :, 0:QKH * HD]
                dve.tensor_tensor(sq[:], qk, qk, ALU.mult).then_inc(prep_step, 1)
                lg = proj[:, :, NPROJ - NE:NPROJ]
                for t in range(T):
                    dve.max(top[:, t, :], lg[:, t, :]).then_inc(prep_step, 1)
                dve.wait_ge(prep_step, at(b, PREP_STEPS, PREP["SQUARES"]))
                dve.tensor_reduce(ms[:], sq[:].rearrange("p t (h e) -> p (t h) e", e=HD), AX.X, ALU.add).then_inc(prep_step, 1)
                for t in range(T):
                    dve.max_index(topi[:, t, :], top[:, t, :], lg[:, t, :]).then_inc(prep_step, 1)
                dve.wait_ge(prep_step, at(b, PREP_STEPS, PREP["SUMS"]))
                dve.tensor_scalar(ms[:], ms[:], 1.0 / HD, RMS_EPS, ALU.mult, ALU.add).then_inc(prep_step, 1)
                dve.tensor_tensor(ldiff[:], top[:, :, 1], top[:, :, 0], ALU.subtract).then_inc(prep_step, 1)
                dve.tensor_copy(topf[:], topi[:, :, 0:2]).then_inc(prep_step, 1)

            def head_rms(b):
                dve.wait_ge(prep_step, at(b, PREP_STEPS, PREP["TOPF"]))
                rsqrt(b, rinv[:], ms[:], rt0[:], rt1[:], PREP["TOPF"])

            def gates(b):
                dve.wait_ge(prep_exp, at(b, 1, 1))
                dve.tensor_scalar(wden[:], eldiff[:], 1.0, None, ALU.add).then_inc(prep_step, 1)
                dve.tensor_scalar(gden[:], egate[:], 1.0, None, ALU.add).then_inc(prep_step, 1)
                dve.wait_ge(prep_step, at(b, PREP_STEPS, PREP["DEN"]))
                dve.reciprocal(wtop[:, 0, :], wden[:]).then_inc(prep_step, 1)
                dve.reciprocal(gsig[:], gden[:]).then_inc(prep_step, 1)
                dve.wait_ge(prep_step, at(b, PREP_STEPS, PREP["WTOP0"]))
                dve.tensor_tensor(wtop[:, 1, :], wtop[:, 0, :], eldiff[:], ALU.mult).then_inc(prep_step, 1)
                for kb in range(2):
                    v = proj[:, kb, D + KV:D + 2 * KV].rearrange("p (g f d) -> p g f d", g=KVH, f=2)
                    s = gsig[:, kb, :].rearrange("p (g f d) -> p g f d", g=KVH, f=2)
                    dve.tensor_tensor(vw_view(b[1], kb, 0, HALF), v, s, ALU.mult).then_inc(v_ready, 1)
                dve.wait_ge(prep_step, at(b, PREP_STEPS, PREP["WTOP1"]))
                for t in range(T):
                    for j, dst in ((0, s0), (1, s1)):
                        dve.tensor_scalar(dst[:, t, :], iota8[:], topf[:, t, j:j + 1], wtop[:, j, t:t + 1],
                                                    ALU.is_equal, ALU.mult).then_inc(prep_step, 1)
                dve.wait_ge(prep_step, at(b, PREP_STEPS, PREP["ONEHOT"]))
                dve.tensor_tensor(score[b[1]][:], s0[:], s1[:], ALU.add).then_inc(prep_step, 1)

            def sT_evacuate(b):
                dve.wait_ge(sT_psum, at(b, 1, 1))
                dve.tensor_copy(scoreT[b[1]][:], misc[0:NE, 0:S]).then_inc(misc_evacuated, 1)

            def rotate(b):
                dve.wait_ge(prep_step, at(b, PREP_STEPS, PREP["RMS_INV"]))
                dve.tensor_tensor(rg[:], rinv[:], qmul[:].rearrange("p t h -> p (t h)"), ALU.mult).then_inc(prep_step, 1)
                dve.wait_ge(prep_step, at(b, PREP_STEPS, PREP["RG"]))
                qk = proj[:, :, 0:QKH * HD].rearrange("p t (h e) -> p t h e", e=HD)
                rgb = rg[:].rearrange("p (t h) -> p t h", t=T).unsqueeze(3).to_broadcast([P, T, QKH, HD])
                dve.tensor_tensor(xr[:], qk, rgb, ALU.mult).then_inc(prep_step, 1)
                dve.wait_ge(prep_step, at(b, PREP_STEPS, PREP["XR"]))
                cosb = cos_sb[:].unsqueeze(2).to_broadcast([P, T, QKH, HD])
                dve.tensor_tensor(ra[:], xr[:], cosb, ALU.mult).then_inc(prep_step, 1)
                for f in range(2):
                    sinb = sin_sb[:, :, f * HALF:(f + 1) * HALF].unsqueeze(2).to_broadcast([P, T, QKH, HALF])
                    dve.tensor_tensor(rb[:, :, :, f * HALF:(f + 1) * HALF],
                                                xr[:, :, :, (1 - f) * HALF:(2 - f) * HALF], sinb, ALU.mult).then_inc(prep_step, 1)
                dve.wait_ge(prep_step, at(b, PREP_STEPS, PREP["ROT"]))
                dve.tensor_tensor(kf[:], ra[:, :, H:QKH, :], rb[:, :, H:QKH, :], ALU.add).then_inc(prep_step, 1)

            def k_parts(b):
                k4 = kf[:].rearrange("p t g (f d) -> p (t g f) d", f=2).unsqueeze(2).to_broadcast([P, T * GF, 2, HALF])
                kv = kp[:].rearrange("p t a (s z) d -> p (t a) s z d", s=2)
                kh, kl = kv[:, :, :, 0, :], kv[:, :, :, 1, :]
                dve.wait_ge(prep_step, at(b, PREP_STEPS, PREP["KF"]))
                dve.tensor_copy(kh, k4).then_inc(prep_step, 1)
                dve.wait_ge(prep_step, at(b, PREP_STEPS, PREP["K_HIGH"]))
                dve.tensor_tensor(kl, k4, kh, ALU.subtract).then_inc(prep_step, 1)

            def q_parts(b):
                for t in range(T):
                    qa, qb = (a[:, t, 0:H, :].rearrange("p (g r) e -> p g r e", g=KVH) for a in (ra, rb))
                    dve.tensor_tensor(qf[:, t].rearrange("p r g e -> p g r e"), qa, qb, ALU.add).then_inc(prep_step, 1)
                n = T * REP * GF
                q4 = qf[:].rearrange("p t r g (f d) -> p (t r g f) d", f=2).unsqueeze(2).to_broadcast([P, n, 2, HALF])
                qv = qp[:].rearrange("p t r a s d -> p (t r a) s d")
                dve.wait_ge(prep_step, at(b, PREP_STEPS, PREP["QF"]))
                dve.tensor_copy(qv[:, :, 0:2, :], q4).then_inc(prep_step, 1)
                dve.wait_ge(prep_step, at(b, PREP_STEPS, PREP["Q_HIGH"]))
                dve.tensor_tensor(qv[:, :, 2:4, :], q4, qv[:, :, 0:2, :], ALU.subtract).then_inc(prep_step, 1)

            def qT_evacuate(b):
                dve.wait_ge(qT_psum, at(b, 1, 1))
                dve.tensor_copy(qT[b[1]][:].rearrange("p r s -> p (r s)"), misc16[:, 0:REP * S]).then_inc(misc_evacuated, 1)

            def kT_evacuate(b, turn):
                dve.wait_ge(kT_psum, at(b, 1, 1))
                dve.tensor_copy(kT[:], misc16[:, 0:S]).then_inc(misc_evacuated, 1)
                dve.wait_ge(misc_evacuated, turn + 2)
                for gf in range(GF):
                    dve.tensor_scalar(kpad[b[1]][:, gf, :], kT[:], gfm_sb[:, gf:gf + 1], None, ALU.mult)\
                       .then_inc(k_ready, 1)

            def exact_maxima(b):
                with dve.If(general_path):
                    for n in range(ROUNDS):
                        dve.wait_ge(max_psum, at(b, ROUNDS + 1, n + 1))
                        t, gfs = (0, (2 * n, 2 * n + 1)) if n < 4 else (1, (n - 4,))
                        m = len(gfs) * REP
                        o = gfs[0] * REP
                        dve.tensor_reduce(nmax[:, t, o:o + m], sbank[0][:].rearrange("p (m w) -> p m w", m=m),
                                          AX.X, ALU.max, negate=True).then_inc(max_read, 1)
                    dve.wait_ge(max_psum, at(b, ROUNDS + 1, ROUNDS + 1))
                    dve.tensor_copy(nmaxT[:], sbank[0][0:32, 0:S]).then_inc(max_read, 1)

            def pv_evacuate(b):
                dve.wait_ge(pv_done, at(b, UNITS, UNITS + RING))
                dve.tensor_copy(pvs[:], pvbank[:]).then_inc(pv_evacuated, 1)

            def normalise(b):
                dve.wait_ge(pvT_psum, at(b, 1, 1))
                v = misc[:].rearrange("p (n e) -> p n e", e=8)
                dve.reciprocal(pinv[:], v[:, :, HALF]).then_inc(tail_step, 1)
                dve.wait_ge(tail_step, at(b, TAIL_STEPS, 1))
                dve.tensor_tensor(an[:].rearrange("p t (n d) -> p (t n) d", d=HALF), v[:, :, 0:HALF],
                                  pinv[:].unsqueeze(2).to_broadcast([P, 64, HALF]), ALU.mult).then_inc(misc_evacuated, 1)

            def aT_evacuate(b):
                dve.wait_ge(aT_psum, at(b, 1, 1))
                dve.tensor_copy(aT[:], misc[:, 0:S]).then_inc(misc_evacuated, 1)

            def final_add(b):
                dve.wait_ge(attn_psum, at(b, 1, 1))
                dve.wait_ge(comb_done, at(b, NE, NE + 1))
                dve.wait_ge(out_stored[b[1]], 16 * b[0] + 16)
                dve.tensor_tensor(ofin[b[1]][:].rearrange("p t d -> p (t d)"), misc[:, 0:S],
                                  acc[b[1]][:].rearrange("p t d -> p (t d)"), ALU.add).then_inc(misc_evacuated, 1)

            def combine(b, e):
                dve.wait_ge(y_psum, at(b, NE, e + 3))
                dve.wait_ge(comb_done, at(b, NE, e + 1))
                for t in range(T):
                    prior = xs[b[1]] if e == 0 else acc[b[1]]
                    last = dve.scalar_tensor_tensor(out=acc[b[1]][:, t, :], in0=ybank[:, t * P:(t + 1) * P],
                                                    scalar=score[b[1]][:, t, e:e + 1], in1=prior[:, t, :],
                                                    op0=ALU.mult, op1=ALU.add)
                last.then_inc(comb_done, 1)

            def seq(b, nxt, prv):
                for k in range(UNITS):
                    if k - 1 in EXPERT_OUT_SLOTS:
                        combine(b, EXPERT_OUT_SLOTS.index(k - 1))
                    if prv is not None:
                        if k == 0:
                            pv_evacuate(prv)
                        if k == TAIL_SLOTS["a_t"] + 1:
                            aT_evacuate(prv)
                        if k == TAIL_SLOTS["attn_out"] + 1:
                            final_add(prv)
                    if nxt is not None:
                        if k == 0:
                            ln_stats(nxt)
                    if k == 0 and prv is not None:
                        normalise(prv)
                    if nxt is not None:
                        if k == 0:
                            ln_apply(nxt)
                        if k == PREP_SLOTS["xn_t"] + 1:
                            xnT_evacuate(nxt)
                        if k == PREP_SLOTS["proj"] + 1:
                            proj_evacuate(nxt, misc_turn("proj", b, prv is not None, True))
                        if k == 5:
                            head_rms(nxt)
                        if k == 6:
                            rotate(nxt)
                            k_parts(nxt)
                        if k == 7:
                            q_parts(nxt)
                        if k == 8:
                            gates(nxt)
                        if k == PREP_SLOTS["k_t"] + 1:
                            kT_evacuate(nxt, misc_turn("k_t", b, prv is not None, True))
                        if k == PREP_SLOTS["q_t"] + 1:
                            qT_evacuate(nxt)
                        if k == PREP_SLOTS["score_t"] + 1:
                            sT_evacuate(nxt)
                            exact_maxima(nxt)
                combine(b, NE - 1)

            general_path = dve.value_load(big_i[0:1, 0:1], min_val=0, max_val=1)
            first = (0, 0)
            ln_stats(first)
            ln_apply(first)
            xnT_evacuate(first)
            proj_evacuate(first, misc_turn("proj", None, False, True))
            head_rms(first)
            rotate(first)
            k_parts(first)
            q_parts(first)
            gates(first)
            kT_evacuate(first, misc_turn("k_t", None, False, True))
            qT_evacuate(first)
            sT_evacuate(first)
            exact_maxima(first)
            schedule(dve, seq)
            pv_evacuate(LAST)
            normalise(LAST)
            aT_evacuate(LAST)
            final_add(LAST)


def tables():
    pos = np.arange(S, dtype=np.float32)
    angles = np.arange(0, HD, 2, dtype=np.float32) / np.float32(HD) * np.float32(math.pi)
    radius = np.float32(1.0) / (np.float32(1.0) + pos[:, None] * np.float32(0.01))
    ang = pos[:, None] * angles[None, :]
    cos, sin = radius * np.cos(ang), radius * np.sin(ang)
    cos_t = np.concatenate([cos, cos], 1).reshape(T, P, HD).transpose(1, 0, 2)
    sin_t = np.concatenate([sin, -sin], 1).reshape(T, P, HD).transpose(1, 0, 2)
    gf_mask = (np.arange(P)[:, None] // 16 == np.arange(GF)[None, :]).astype(np.float32)
    ident = np.eye(P, dtype=np.float32)
    causal = np.where(np.arange(P)[None, :] > np.arange(P)[:, None], NEG, 0.0).astype(np.float32)
    return cos_t, sin_t, gf_mask, ident, causal


def kernel(L0_attn_x, L0_attn_Wq, L0_attn_Wk, L0_attn_Wv, L0_attn_Wg, L0_attn_Wo, L0_attn_q_gain,
           L0_attn_lambda_param, L0_ffn_Wg, L0_ffn_W1, L0_ffn_b1, L0_ffn_W2, L0_ffn_b2):
    import concourse.bacc as _bacc
    from concourse.bass_utils import run_bass_kernel_spmd as _run

    a = np.asarray
    cos_t, sin_t, gf_mask, ident, causal = tables()
    w_proj = np.concatenate([a(L0_attn_Wq).T, a(L0_attn_Wk).T, a(L0_attn_Wv).T, a(L0_attn_Wg).T, a(L0_ffn_Wg)], axis=1)
    wo = a(L0_attn_Wo).T.reshape(KVH, REP, 2, HALF, D).transpose(2, 1, 0, 3, 4).reshape(2, D // 2, D)
    lam = np.repeat(a(L0_attn_lambda_param).reshape(KVH, REP).T.reshape(H), HALF)[:, None]
    arrays = {
        "x": a(L0_attn_x),
        "w_proj": w_proj,
        "wo_a": np.concatenate([wo[0], wo[0]]),
        "wo_b": np.concatenate([wo[1], wo[1]]),
        "gain": np.broadcast_to(a(L0_attn_q_gain)[None, :], (P, H)),
        "lam_col": np.concatenate([np.ones((D // 2, 1), np.float32), lam]),
        "w1": a(L0_ffn_W1).transpose(1, 0, 2),
        "b1": a(L0_ffn_b1).reshape(NE, HC, P).transpose(2, 0, 1),
        "w2": a(L0_ffn_W2).reshape(NE, HC, P, D).transpose(2, 0, 1, 3),
        "b2": a(L0_ffn_b2),
        "cos_t": cos_t,
        "sin_t": sin_t,
        "gf_mask": gf_mask,
        "ident": ident,
        "causal_neg": causal,
    }
    arrays = {n: np.ascontiguousarray(v) for n, v in arrays.items()}
    nc = _bacc.Bacc("TRN2", target_bir_lowering=False, num_devices=1)
    args = {n: nc.dram_tensor(f"in_{n}", v.shape, mybir.dt.from_np(v.dtype), kind="ExternalInput").ap()
            for n, v in arrays.items()}
    out = nc.dram_tensor("out_y", (NB, S, D), F32, kind="ExternalOutput").ap()
    moe_attention_kernel(nc, out=out, **args)
    r = _run(nc, [{f"in_{n}": v for n, v in arrays.items()}], core_ids=[0])
    return r.results[0]["out_y"]
```

```python
import math
from contextlib import ExitStack

import numpy as np

import concourse.bass as bass
from concourse import mybir

F32 = mybir.dt.float32
F16 = mybir.dt.float16
BF16 = mybir.dt.bfloat16
I32 = mybir.dt.int32
U32 = mybir.dt.uint32
ALU = mybir.AluOpType
ACT = mybir.ActivationFunctionType
AX = mybir.AxisListType

P = 128
NB, S, D = 32, 256, 128
T = S // P
H, KVH = 16, 4
HD = D // H
HALF = HD // 2
REP = H // KVH
KV = KVH * HD
GF = KVH * 2
NE, HID = 8, 256
HC = HID // P
NPROJ = D + 3 * KV + NE
QKH = H + KVH
UNITS = 12
UW = 1024
RING = 4
LN_EPS = 1e-5
RMS_EPS = float(np.finfo(np.float32).eps)
SCALE = 1.0 / math.sqrt(HALF)
EXP_BIT = 1 << 23
F16_TOP = 14
TINY_MAX = 2.0 ** -40
RSQRT_MAGIC = 0x5F3759DF
GAIN_LIMIT = 8.0
NEG = -3.0e38

NEWTON = 3 * 3
_stages = {
    "STATS": T, "VAR_IN": 1 + T, "VAR": 1, "XN": T,
    "SQUARES": 1 + T, "SUMS": 1 + T, "MS": 1, "LDIFF": 1, "TOPF": 1, "RMS_GUESS": 3, "RMS_INV": NEWTON,
    "RG": 2, "XR": 1, "ROT": 3, "KF": 1, "K_HIGH": 1, "KP": 1, "QF": T, "Q_HIGH": 1, "QP": 1,
    "DEN": 2, "WTOP0": 2, "WTOP1": 1, "WEIGHTED": 1, "SCORE": 1, "YSCORE": 1,
}
PREP = dict(zip(_stages, (int(n) for n in np.cumsum(list(_stages.values())))))
PREP_STEPS = PREP["YSCORE"]
TAIL_STEPS = 1
SETUP_STEPS = 49
FIRST_SETUP = 34
SMALL = 12 * 16
EXPERTS = 2 * 16

UNIT = []
for _f in range(2):
    for _pair in range(KVH // 2):
        _g = 2 * _pair
        UNIT += [(_f, 0, (_g,)), (_f, 0, (_g + 1,)), (_f, 1, (_g, _g + 1))]
assert len(UNIT) == UNITS

TAIL_SLOTS = {"pv_t": 0, "a_t": 3, "attn_out": 4}
PREP_SLOTS = {"xn_t": 1, "proj": 2, "k_t": 7, "q_t": 8, "score_t": 10}
HALVES = 2 * UNITS
EXPERT_IN_HALVES = [HALVES // NE * e for e in range(NE)]
EXPERT_OUT_HALVES = [h + 7 for h in EXPERT_IN_HALVES]
EXPERT_IN_SLOTS = [h // 2 for h in EXPERT_IN_HALVES]
LATE_EXPERTS = [e for e in range(NE) if EXPERT_OUT_HALVES[e] >= HALVES]
LATE_SPLITS = [e for e in range(NE) if EXPERT_IN_SLOTS[e] + 2 >= UNITS]
SPLIT_SLOTS = [s + 2 for s in EXPERT_IN_SLOTS]
H_RING = 4
MISC_ORDER = ["pv_t", "xn_t", "proj", "a_t", "attn_out", "k_t", "q_t", "score_t"]
ROUNDS = 12


LAST = (NB // 2 - 1, 1)


def at(b, per, k):
    return (2 * per) * b[0] + (per * b[1] + k)


def after(b):
    return b[0] + b[1], 1 - b[1]


def before(b):
    return b[0] - (1 - b[1]), 1 - b[1]


def moe_attention_kernel(nc, x, w_proj, wo_a, wo_b, gain, lam_col, w1, b1, w2, b2, cos_t, sin_t, gf_mask, ident, causal_neg, out):
    ctx = ExitStack()
    with ctx:
        def sb(name, shape, dt=F32):
            return ctx.enter_context(nc.sbuf_tensor(name, shape, dt))

        def pb(name, shape, dt=F32):
            return ctx.enter_context(nc.psum_tensor(name, shape, dt))

        def sem(name):
            return ctx.enter_context(nc.semaphore(name))

        wproj_sb = sb("wproj_sb", [P, NPROJ])
        woa_sb = sb("woa_sb", [P, D])
        wob_sb = sb("wob_sb", [P, D])
        wo_sb = sb("wo_sb", [P, D])
        w1h = sb("w1h", [P, NE, HID], F16)
        w1l = sb("w1l", [P, NE, HID], F16)
        w2h = sb("w2h", [P, NE, HC, D], F16)
        w2l = sb("w2l", [P, NE, HC, D], F16)
        b1s = sb("b1s", [P, NE, HC])
        peak = sb("peak", [P, 3])
        peak_all = sb("peak_all", [3, 1])
        peak_diag = sb("peak_diag", [3, 3])
        ones3 = sb("ones3", [3, P])
        bound = sb("bound", [P, 3])
        bound_e = sb("bound_e", [P, 3], I32)
        up = sb("up", [P, 3])
        down = sb("down", [P, 3])
        h_scale = sb("h_scale", [P, 1])
        y_scale = sb("y_scale", [P, 1])
        lamc = sb("lamc", [P, 1])
        lamn = sb("lamn", [P, 1])
        w1_sb = sb("w1_sb", [P, NE, HID])
        b1_sb = sb("b1_sb", [P, NE, HC])
        w2_sb = sb("w2_sb", [P, NE, HC, D])
        b2_sb = sb("b2_sb", [NE, D])
        cos_sb = sb("cos_sb", [P, T, HD])
        sin_sb = sb("sin_sb", [P, T, HD])
        gfm_sb = sb("gfm_sb", [P, GF])
        id32 = sb("id32", [P, P])
        id16 = sb("id16", [P, P], F16)
        idb = sb("idb", [P, P], BF16)
        neg32 = sb("neg32", [P, P])
        negb = sb("negb", [P, P], BF16)
        gain_sb = sb("gain_sb", [P, H])
        gabs = sb("gabs", [P, H])
        gmax = sb("gmax", [P, 1])
        big = sb("big", [P, 1])
        big_i = sb("big_i", [P, 1], I32)
        gsgn = sb("gsgn", [P, H])
        gtmp = sb("gtmp", [P, H])
        qmul = sb("qmul", [P, T, QKH])
        iota8 = sb("iota8", [P, NE])
        rt0 = sb("rt0", [P, T * QKH])
        rt1 = sb("rt1", [P, T * QKH])

        xs = [sb(f"xs{i}", [P, T, D]) for i in range(2)]
        stats = sb("stats", [P, T, 6])
        mhalf = sb("mhalf", [P, T])
        mv = sb("mv", [P, T, 2])
        vare = sb("vare", [P, T])
        rstd = sb("rstd", [P, T])
        xn = sb("xn", [P, T, D])
        xnT = sb("xnT", [P, S])
        xnTh = [sb(f"xnTh{i}", [P, S], F16) for i in range(2)]
        xnTl = [sb(f"xnTl{i}", [P, S], F16) for i in range(2)]
        proj = sb("proj", [P, T, NPROJ])
        sq = sb("sq", [P, T, QKH * HD])
        ms = sb("ms", [P, T * QKH])
        rinv = sb("rinv", [P, T * QKH])
        rg = sb("rg", [P, T * QKH])
        xr = sb("xr", [P, T, QKH, HD])
        ra = sb("ra", [P, T, QKH, HD])
        rb = sb("rb", [P, T, QKH, HD])
        qf = sb("qf", [P, T, REP, KVH, HD])
        kf = sb("kf", [P, T, KVH, HD])
        qp = sb("qp", [P, T, REP, GF, 4, HALF], F16)
        kp = sb("kp", [P, T, GF, 4, HALF], F16)
        qT = [sb(f"qT{i}", [P, REP, S], F16) for i in range(2)]
        kT = sb("kT", [P, S], F16)
        kpad = [sb(f"kpad{i}", [P, GF, S], F16) for i in range(2)]
        egate = sb("egate", [P, T, KV])
        gden = sb("gden", [P, T, KV])
        gsig = sb("gsig", [P, T, KV])
        vw = [sb(f"vw{i}", [P, 2 * GF * 32 + 32]) for i in range(2)]
        top = sb("top", [P, T, 8])
        topi = sb("topi", [P, T, 8], U32)
        topf = sb("topf", [P, T, 2])
        ldiff = sb("ldiff", [P, T])
        eldiff = sb("eldiff", [P, T])
        wden = sb("wden", [P, T])
        wtop = sb("wtop", [P, 2, T])
        chosen = sb("chosen", [P, 2, T, NE])
        score = [sb(f"score{i}", [P, T, NE]) for i in range(2)]
        yscore = [sb(f"yscore{i}", [P, T, NE]) for i in range(2)]
        scoreT = [sb(f"scoreT{i}", [NE, S]) for i in range(2)]
        probs = [sb(f"probs{i}", [P, UW]) for i in range(RING)]
        h32 = [sb(f"h32_{i}", [P, HC, S]) for i in range(H_RING)]
        hh = [sb(f"hh{i}", [P, HC, S], F16) for i in range(H_RING)]
        hl = [sb(f"hl{i}", [P, HC, S], F16) for i in range(H_RING)]
        acc = [sb(f"acc{i}", [P, T, D]) for i in range(2)]
        pvs = sb("pvs", [P, 2, S])
        pinv = sb("pinv", [P, 64])
        an = sb("an", [P, T, D])
        aT = sb("aT", [P, S])
        ofin = [sb(f"ofin{i}", [P, T, D]) for i in range(2)]
        nmax = sb("nmax", [P, T, 32])
        nmaxT = sb("nmaxT", [32, S])
        credits = sb("credits", [P, 16])
        hold = sb("hold", [P, 1])

        sbank = [pb(f"sbank{i}", [P, UW]) for i in range(2)]
        pvbank = pb("pvbank", [P, 2, S])
        hbank = pb("hbank", [P, HC, S])
        ybank = pb("ybank", [P, 512])
        misc = pb("misc", [P, 512])
        misc16 = misc[:, :].bitcast(F16)

        def vw_view(p, kb, c0, c1):
            flat = vw[p][:, kb * 256:kb * 256 + 288].rearrange("p (g x) -> p g x", g=KVH)
            return flat[:, :, 0:64].rearrange("p g (f y) -> p g f y", f=2)[:, :, :, c0:c1]

        weights_in = sem("weights_in")
        experts_in = sem("experts_in")
        x_in = [sem(f"x_in{i}") for i in range(2)]
        out_stored = [sem(f"out_stored{i}") for i in range(2)]
        setup = sem("setup")
        prep_step = sem("prep_step")
        tail_step = sem("tail_step")
        ln_rstd = sem("ln_rstd")
        prep_exp = sem("prep_exp")
        xn_high = sem("xn_high")
        xn_low = sem("xn_low")
        v_ready = sem("v_ready")
        k_ready = sem("k_ready")
        xnT_psum = sem("xnT_psum")
        proj_psum = sem("proj_psum")
        sT_psum = sem("sT_psum")
        qT_psum = sem("qT_psum")
        kT_psum = sem("kT_psum")
        pvT_psum = sem("pvT_psum")
        aT_psum = sem("aT_psum")
        attn_psum = sem("attn_psum")
        misc_evacuated = sem("misc_evacuated")
        scores_ready = sem("scores_ready")
        exp_done = [sem(f"exp_done{i}") for i in range(RING)]
        mask_done = sem("mask_done")
        pv_done = sem("pv_done")
        pv_evacuated = sem("pv_evacuated")
        h_psum = sem("h_psum")
        relu_done = sem("relu_done")
        high_done = sem("high_done")
        low_done = sem("low_done")
        peak_psum = sem("peak_psum")
        w_high = sem("w_high")
        w_split = sem("w_split")
        y_psum = sem("y_psum")
        comb_done = sem("comb_done")
        max_psum = sem("max_psum")
        max_read = sem("max_read")

        block = ctx.enter_context(nc.Block())

        def misc_turn(step, b, tail, prep, past=False):
            kinds = [k for k in MISC_ORDER if (k in TAIL_SLOTS and tail) or (k in PREP_SLOTS and prep)]
            n = kinds.index(step)
            if b is None:
                return n
            if not tail:
                return len(PREP_SLOTS) + n
            return at(b, len(MISC_ORDER), 2 * len(PREP_SLOTS) - len(MISC_ORDER) + n + (len(TAIL_SLOTS) if past else 0))

        def schedule(eng, seq):
            a, z = (0, 0), (0, 1)
            seq(a, z, None)
            seq(z, after(z), a)
            with eng.Fori(1, NB // 2 - 1) as i:
                for p in range(2):
                    b = (i, p)
                    seq(b, after(b), before(b))
            a, z = (NB // 2 - 1, 0), (NB // 2 - 1, 1)
            seq(a, z, before(a))
            seq(z, None, a)

        @block.sync
        def _(sp):
            xr_ = x.rearrange("b (t p) d -> b p t d", p=P)
            or_ = out.rearrange("b (t p) d -> b p t d", p=P)
            sp.dma_start(xs[0][:], xr_[0]).then_inc(x_in[0], 16)
            for dst, src in ((wproj_sb[:], w_proj), (id32[:], ident), (gain_sb[:], gain), (cos_sb[:], cos_t),
                             (sin_sb[:], sin_t), (gfm_sb[:], gf_mask), (neg32[:], causal_neg),
                             (woa_sb[:], wo_a), (wob_sb[:], wo_b), (lamc[:], lam_col), (b1_sb[:], b1),
                             (b2_sb[:], b2)):
                sp.dma_start(dst, src).then_inc(weights_in, 16)
            for dst, src in ((w1_sb[:], w1), (w2_sb[:], w2)):
                sp.dma_start(dst, src).then_inc(experts_in, 16)
            sp.dma_start(xs[1][:], xr_[1]).then_inc(x_in[1], 16)

            def store(b, turn):
                sp.wait_ge(misc_evacuated, turn + 2)
                sp.dma_start(or_[2 * b[0] + b[1]], ofin[b[1]][:]).then_inc(out_stored[b[1]], 16)

            def seq(b, nxt, prv):
                if prv is not None:
                    store(prv, misc_turn("attn_out", b, True, nxt is not None))
                if not (isinstance(b[0], int) and b[0] == NB // 2 - 1):
                    sp.wait_ge(comb_done, at(b, NE, 2))
                    sp.dma_start(xs[b[1]][:], xr_[2 * b[0] + (b[1] + 2)]).then_inc(x_in[b[1]], 16)

            schedule(sp, seq)
            store(LAST, misc_turn("attn_out", LAST, True, False, past=True))
            for p in range(2):
                sp.wait_ge(out_stored[p], 16 * (NB // 2 + 1))

        @block.tensor
        def _(pe):
            def xn_transposes(b, turn):
                pe.wait_ge(misc_evacuated, turn + 1)
                pe.wait_ge(prep_step, at(b, PREP_STEPS, PREP["XN"]))
                for t in range(T):
                    last = pe.transpose(misc[:, t * P:(t + 1) * P], xn[:, t, :], id32[:])
                last.then_inc(xnT_psum, 1)

            def projection(b, turn):
                pe.wait_ge(misc_evacuated, turn + 1)
                for t in range(T):
                    last = pe.matmul(misc[:, t * NPROJ:(t + 1) * NPROJ], xnT[:, t * P:(t + 1) * P],
                                     wproj_sb[:], start=True, stop=True)
                last.then_inc(proj_psum, 1)

            def score_transposes(b, turn):
                pe.wait_ge(misc_evacuated, turn + 1)
                pe.wait_ge(prep_step, at(b, PREP_STEPS, PREP["SCORE"]))
                for t in range(T):
                    last = pe.transpose(misc[0:NE, t * P:(t + 1) * P], score[b[1]][:, t, :], id32[:])
                last.then_inc(sT_psum, 1)

            def q_transposes(b, turn):
                pe.wait_ge(misc_evacuated, turn + 1)
                pe.wait_ge(prep_step, at(b, PREP_STEPS, PREP["QP"]))
                for r in range(REP):
                    for t in range(T):
                        o = (r * T + t) * P
                        last = pe.transpose(misc16[:, o:o + P], qp[:, t, r].rearrange("p a b c -> p (a b c)"), id16[:])
                last.then_inc(qT_psum, 1)

            def k_transposes(b, turn):
                pe.wait_ge(misc_evacuated, turn + 1)
                pe.wait_ge(prep_step, at(b, PREP_STEPS, PREP["KP"]))
                for t in range(T):
                    last = pe.transpose(misc16[:, t * P:(t + 1) * P], kp[:, t].rearrange("p a b c -> p (a b c)"), id16[:])
                last.then_inc(kT_psum, 1)

            def pv_transposes(b, turn):
                pe.wait_ge(misc_evacuated, turn + 1)
                pe.wait_ge(pv_evacuated, at(b, 1, 2))
                for t in range(T):
                    for f in range(2):
                        o = (t * 2 + f) * P
                        last = pe.transpose(misc[:, o:o + P], pvs[:, f, t * P:(t + 1) * P], id32[:])
                last.then_inc(pvT_psum, 1)

            def a_transposes(b, turn):
                pe.wait_ge(misc_evacuated, turn + 1)
                for t in range(T):
                    last = pe.transpose(misc[:, t * P:(t + 1) * P], an[:, t, :], id32[:])
                last.then_inc(aT_psum, 1)

            def attention_out(b, turn):
                pe.wait_ge(misc_evacuated, turn + 1)
                for t in range(T):
                    o = misc[:, t * P:(t + 1) * P]
                    pe.matmul(o, aT[:, t * P:(t + 1) * P], wo_sb[:], start=True, stop=False)
                    last = pe.matmul(o, scoreT[b[1]][:, t * P:(t + 1) * P], b2_sb[:], start=False, stop=True)
                last.then_inc(attn_psum, 1)

            def score_unit(b, u, general):
                f, kb, gs = UNIT[u]
                bank = sbank[u % 2]
                for n in range(2):
                    if kb == 0:
                        rhs, g = qT[b[1]][:, 2 * n:2 * n + 2, :], gs[0]
                    else:
                        rhs, g = qT[b[1]][:, :, P:S], gs[n]
                    gf = 2 * g + f
                    o = bank[:, n * 512:(n + 1) * 512]
                    last = pe.matmul(o, kpad[b[1]][:, gf, kb * P:(kb + 1) * P], rhs, start=True, stop=not general,
                                     skip_group_check=general)
                    if general:
                        heads = (2 * n, 2 * n + 1) if kb == 0 else range(REP)
                        w = S // (kb + 1)
                        for j, r in enumerate(heads):
                            hh = gf * REP + r
                            last = pe.matmul(o[:, j * w:(j + 1) * w], id32[0:32, hh:hh + 1].to_broadcast([32, P]),
                                             nmaxT[:, kb * P:S], start=False, stop=True, skip_group_check=True)
                last.then_inc(scores_ready, 1)

            def scores(b, u, general, turn=None):
                pe.wait_ge(mask_done, at(b, UNITS, u + 1))
                if turn is not None:
                    pe.wait_ge(misc_evacuated, turn + 2)
                    pe.wait_ge(k_ready, at(b, GF, GF))
                score_unit(b, u, general)

            def exact_maxima(b, current, turn):
                pe.wait_ge(misc_evacuated, turn + 2)
                pe.wait_ge(k_ready, at(b, GF, GF))
                if current is not None:
                    pe.wait_ge(mask_done, at(current, UNITS, UNITS + 1))
                for n in range(ROUNDS):
                    pe.wait_ge(max_read, at(b, ROUNDS + 1, n + 1))
                    t, gfs = (0, (2 * n, 2 * n + 1)) if n < 4 else (1, (n - 4,))
                    w = (t + 1) * P
                    for j, gf in enumerate(gfs):
                        for r in range(REP):
                            o = sbank[0][:, (j * REP + r) * w:(j * REP + r + 1) * w]
                            pe.matmul(o, qT[b[1]][:, r, t * P:(t + 1) * P], kpad[b[1]][:, gf, 0:w],
                                      start=True, stop=False, skip_group_check=True)
                            last = pe.matmul(o[:, t * P:w], idb[:], negb[:], start=False, stop=True,
                                             skip_group_check=True)
                    last.then_inc(max_psum, 1)
                pe.wait_ge(max_read, at(b, ROUNDS + 1, ROUNDS + 1))
                for t in range(T):
                    last = pe.transpose(sbank[0][0:32, t * P:(t + 1) * P], nmax[:, t, :], id32[:])
                last.then_inc(max_psum, 1)
                pe.wait_ge(max_read, at(b, ROUNDS + 1, ROUNDS + 2))

            def values(b, u):
                f, kb, gs = UNIT[u]
                pe.wait_ge(mask_done, at(b, UNITS, u + 3))
                if u == 0:
                    pe.wait_ge(v_ready, at(b, 2, 2))
                    pe.wait_ge(pv_evacuated, at(b, 1, 1))
                for n, g in enumerate(gs):
                    gf = 2 * g + f
                    for r in range(REP):
                        w = S // (kb + 1)
                        rhs = probs[u % RING][:, (n * REP + r) * w:(n * REP + r + 1) * w]
                        last = pe.matmul(pvbank[32 * r:32 * r + 32, f, kb * P:S],
                                         vw[b[1]][:, (kb * GF + gf) * 32:(kb * GF + gf + 1) * 32], rhs,
                                         start=(g == 0 and kb == 0), stop=(g == KVH - 1 and kb == 1),
                                         skip_group_check=True)
                last.then_inc(pv_done, 1)

            def expert_in(b, e):
                pe.wait_ge(relu_done, at(b, NE, e + 1))
                if e == 0:
                    pe.wait_ge(xn_low, at(b, 1, 1))
                for c in range(HC):
                    o, wh, wl = hbank[:, c, :], w1h[:, e, c * P:(c + 1) * P], w1l[:, e, c * P:(c + 1) * P]
                    pe.matmul(o, wl, xnTh[b[1]][:], start=True, stop=False)
                    pe.matmul(o, wh, xnTh[b[1]][:], start=False, stop=False)
                    last = pe.matmul(o, wh, xnTl[b[1]][:], start=False, stop=True)
                last.then_inc(h_psum, 1)

            def expert_out(b, e):
                pe.wait_ge(low_done, at(b, NE, e + 1))
                pe.wait_ge(comb_done, at(b, NE, e + 1))
                for t in range(T):
                    o, tok = ybank[:, t * P:(t + 1) * P], slice(t * P, (t + 1) * P)
                    for c in range(HC):
                        pe.matmul(o, hh[e % H_RING][:, c, tok], w2h[:, e, c, :], start=(c == 0), stop=False)
                        pe.matmul(o, hh[e % H_RING][:, c, tok], w2l[:, e, c, :], start=False, stop=False)
                        last = pe.matmul(o, hl[e % H_RING][:, c, tok], w2h[:, e, c, :], start=False, stop=(c == HC - 1))
                last.then_inc(y_psum, 1)

            def experts(b, prv, half):
                if half in EXPERT_OUT_HALVES:
                    expert_out(b, EXPERT_OUT_HALVES.index(half))
                if prv is not None and half + HALVES in EXPERT_OUT_HALVES:
                    expert_out(prv, EXPERT_OUT_HALVES.index(half + HALVES))
                if half in EXPERT_IN_HALVES:
                    expert_in(b, EXPERT_IN_HALVES.index(half))

            def seq(b, nxt, prv, general):
                for u in range(UNITS):
                    if u < UNITS - 1:
                        scores(b, u + 1, general)
                    elif nxt is not None:
                        turn = misc_turn("q_t", b, prv is not None, True)
                        if general:
                            exact_maxima(nxt, b, turn)
                        scores(nxt, 0, general, turn)
                    experts(b, prv, 2 * u)
                    for name in MISC_ORDER:
                        if prv is not None and u == TAIL_SLOTS.get(name):
                            tail_steps[name](prv, misc_turn(name, b, True, nxt is not None))
                        if nxt is not None and u == PREP_SLOTS.get(name):
                            prep_steps[name](nxt, misc_turn(name, b, prv is not None, True))
                    values(b, u)
                    experts(b, prv, 2 * u + 1)

            prep_steps = {"xn_t": xn_transposes, "proj": projection, "k_t": k_transposes, "q_t": q_transposes,
                          "score_t": score_transposes}
            tail_steps = {"pv_t": pv_transposes, "a_t": a_transposes, "attn_out": attention_out}
            pe.wait_ge(weights_in, SMALL)
            pe.wait_ge(setup, FIRST_SETUP)
            general_path = pe.value_load(big_i[0:1, 0:1], min_val=0, max_val=1)
            for name, step in prep_steps.items():
                step((0, 0), misc_turn(name, None, False, True))
            pe.wait_ge(setup, FIRST_SETUP + 4)
            pe.transpose(hbank[0:3, 0, 0:P], peak[:], id32[:]).then_inc(peak_psum, 1)
            pe.wait_ge(setup, FIRST_SETUP + 6)
            pe.matmul(hbank[:, 1, 0:3], ones3[:], peak_diag[:], start=True, stop=True).then_inc(peak_psum, 1)

            def all_sequences(general):
                turn = misc_turn("q_t", None, False, True)
                if general:
                    exact_maxima((0, 0), None, turn)
                scores((0, 0), 0, general, turn)
                pe.wait_ge(w_split, 2)
                schedule(pe, lambda b, nxt, prv: seq(b, nxt, prv, general))

            with pe.If(general_path):
                all_sequences(True)
            with pe.Else():
                all_sequences(False)
            for e in LATE_EXPERTS:
                expert_out(LAST, e)
            for name, step in tail_steps.items():
                step(LAST, misc_turn(name, LAST, True, False, past=True))

        @block.scalar
        def _(act):
            def exps(b, u, general):
                act.wait_ge(pv_done, at(b, UNITS, u + 1))
                act.wait_ge(scores_ready, at(b, UNITS, u + 1))
                f, kb, gs = UNIT[u]
                dst, src = probs[u % RING], sbank[u % 2]
                if general:
                    w = S // (kb + 1)
                    for n, g in enumerate(gs):
                        for r in range(REP):
                            a, h = (n * REP + r) * w, g * REP + r
                            last = nc.scalar.activation(dst[:, a:a + w], src[:, a:a + w], ACT.Exp,
                                                        scale=gabs[:, h:h + 1])
                    last.then_inc(exp_done[u % RING], 1)
                else:
                    nc.scalar.activation(dst[:], src[:], ACT.Exp).then_inc(exp_done[u % RING], 1)

            def relus(b, e):
                act.wait_ge(h_psum, at(b, NE, e + 1))
                act.wait_ge(y_psum, at(b, NE, e + 1))
                for c in range(HC):
                    last = nc.scalar.activation(h32[e % H_RING][:, c, :], hbank[:, c, :], ACT.Relu,
                                                bias=b1s[:, e, c:c + 1], scale=h_scale[:, 0:1])
                last.then_inc(relu_done, 1)

            def high_part(b, e):
                act.wait_ge(relu_done, at(b, NE, e + 2))
                nc.scalar.activation(hh[e % H_RING][:], h32[e % H_RING][:], ACT.Copy).then_inc(high_done, 1)

            def prep_exps(b):
                act.wait_ge(prep_step, at(b, PREP_STEPS, PREP["LDIFF"]))
                nc.scalar.activation(egate[:], proj[:, :, D + 2 * KV:D + 3 * KV], ACT.Exp, scale=-1.0)
                nc.scalar.activation(eldiff[:], ldiff[:], ACT.Exp).then_inc(prep_exp, 1)

            def seq(b, nxt, prv, general):
                for u in range(UNITS):
                    exps(b, u, general)
                    if u in SPLIT_SLOTS:
                        high_part(b, SPLIT_SLOTS.index(u))
                    if prv is not None and u + UNITS in SPLIT_SLOTS:
                        high_part(prv, SPLIT_SLOTS.index(u + UNITS))
                    if u - 1 in EXPERT_IN_SLOTS:
                        relus(b, EXPERT_IN_SLOTS.index(u - 1))
                    if u == 6 and nxt is not None:
                        prep_exps(nxt)

            act.wait_ge(weights_in, SMALL)
            act.wait_ge(setup, FIRST_SETUP)
            general_path = act.value_load(big_i[0:1, 0:1], min_val=0, max_val=1)
            prep_exps((0, 0))
            act.wait_ge(experts_in, EXPERTS)
            act.wait_ge(setup, SETUP_STEPS)
            nc.scalar.activation(w1h[:], w1_sb[:], ACT.Copy, scale=up[:, 0:1]).then_inc(w_high, 1)
            nc.scalar.activation(w2h[:], w2_sb[:], ACT.Copy, scale=up[:, 1:2]).then_inc(w_high, 1)
            with act.If(general_path):
                schedule(act, lambda b, nxt, prv: seq(b, nxt, prv, True))
            with act.Else():
                schedule(act, lambda b, nxt, prv: seq(b, nxt, prv, False))
            for e in LATE_SPLITS:
                high_part(LAST, e)

        @block.gpsimd
        def _(pool):
            def masks(b, u):
                f, kb, gs = UNIT[u]
                pool.wait_ge(exp_done[u % RING], 1)
                pool.sem_clear(exp_done[u % RING])
                if kb == 0:
                    v = probs[u % RING][:].rearrange("p (r q) -> p r q", r=REP)[:, :, 0:P]
                    n = REP
                else:
                    v = probs[u % RING][:].rearrange("p (r q) -> p r q", r=2 * REP)
                    n = 2 * REP
                nc.gpsimd.affine_select(out=v, in_=v, compare_op=ALU.is_ge, fill=0.0, base=0,
                                        pattern=[[0, n], [1, P]], channel_multiplier=-1).then_inc(mask_done, 1)

            def low_parts(b, e):
                pool.wait_ge(high_done, at(b, NE, e + 1))
                nc.gpsimd.tensor_tensor(hl[e % H_RING][:], h32[e % H_RING][:], hh[e % H_RING][:], ALU.subtract).then_inc(low_done, 1)

            def layer_rstd(b):
                pool.wait_ge(prep_step, at(b, PREP_STEPS, PREP["VAR"]))
                nc.gpsimd.tensor_tensor(rstd[:], vare[:], mhalf[:], ALU.pow).then_inc(ln_rstd, 1)

            def seq(b, nxt, prv):
                for u in range(UNITS):
                    if u == 0 and nxt is not None:
                        layer_rstd(nxt)
                    masks(b, u)
                    if u in SPLIT_SLOTS:
                        low_parts(b, SPLIT_SLOTS.index(u))
                    if prv is not None and u + UNITS in SPLIT_SLOTS:
                        low_parts(prv, SPLIT_SLOTS.index(u + UNITS))

            pool.wait_ge(setup, FIRST_SETUP)
            layer_rstd((0, 0))
            schedule(pool, seq)
            for e in LATE_SPLITS:
                low_parts(LAST, e)

        @block.vector
        def _(dve):
            dve.wait_ge(weights_in, SMALL)
            dve.tensor_copy(id16[:], id32[:]).then_inc(setup, 1)
            dve.tensor_copy(idb[:], id32[:]).then_inc(setup, 1)
            dve.tensor_copy(negb[:], neg32[:]).then_inc(setup, 1)
            for j in range(NE):
                dve.memset(iota8[:, j:j + 1], float(j)).then_inc(setup, 1)
            for p in range(2):
                dve.memset(vw[p][:], 0.0).then_inc(setup, 1)
            dve.wait_ge(setup, 13)
            for p in range(2):
                for kb in range(2):
                    dve.memset(vw_view(p, kb, HALF, HALF + 1), 1.0).then_inc(setup, 1)
            dve.tensor_scalar(gtmp[:], gain_sb[:], -1.0, None, ALU.mult).then_inc(setup, 1)
            dve.wait_ge(setup, 18)
            dve.tensor_tensor(gabs[:], gtmp[:], gain_sb[:], ALU.max).then_inc(setup, 1)
            dve.wait_ge(setup, 19)
            dve.tensor_reduce(gmax[:], gabs[:], AX.X, ALU.max).then_inc(setup, 1)
            dve.tensor_scalar(gsgn[:], gain_sb[:], 0.0, 2.0, ALU.is_ge, ALU.mult).then_inc(setup, 1)
            dve.wait_ge(setup, 21)
            dve.tensor_scalar(big[:], gmax[:], GAIN_LIMIT, None, ALU.is_gt).then_inc(setup, 1)
            dve.scalar_tensor_tensor(out=gtmp[:], in0=gsgn[:], scalar=-1.0, in1=gain_sb[:], op0=ALU.add, op1=ALU.subtract).then_inc(setup, 1)
            dve.wait_ge(setup, 23)
            dve.tensor_copy(big_i[:], big[:]).then_inc(setup, 1)
            dve.scalar_tensor_tensor(out=gsgn[:], in0=gtmp[:], scalar=big[:, 0:1], in1=gain_sb[:], op0=ALU.mult, op1=ALU.add).then_inc(setup, 1)
            dve.wait_ge(setup, 25)
            for t in range(T):
                dve.tensor_scalar(qmul[:, t, 0:H], gsgn[:], SCALE, None, ALU.mult).then_inc(setup, 1)
                dve.memset(qmul[:, t, H:QKH], 1.0).then_inc(setup, 1)
            dve.tensor_scalar(lamn[0:64, :], lamc[0:64, :], 1.0, None, ALU.mult).then_inc(setup, 1)
            dve.tensor_scalar(lamn[64:P, :], lamc[64:P, :], -1.0, None, ALU.mult).then_inc(setup, 1)
            dve.wait_ge(setup, 31)
            dve.tensor_scalar(wo_sb[:], woa_sb[:], lamn[:, 0:1], None, ALU.mult).then_inc(setup, 1)
            dve.wait_ge(setup, 32)
            dve.scalar_tensor_tensor(out=wo_sb[:], in0=wob_sb[:], scalar=lamc[:, 0:1], in1=wo_sb[:], op0=ALU.mult, op1=ALU.add).then_inc(setup, 1)
            dve.memset(mhalf[:], -0.5).then_inc(setup, 1)
            dve.wait_ge(setup, FIRST_SETUP)
            n_credit = 0
            for s, v in ((misc_evacuated, 1), (mask_done, 2), (pv_done, RING), (pv_evacuated, 1), (relu_done, 1),
                         (y_psum, H_RING), (comb_done, 1), (max_read, 1), (out_stored[0], 16), (out_stored[1], 16)):
                dve.memset(credits[:, n_credit:n_credit + 1], 0.0).then_inc(s, v)
                n_credit += 1

            def ln_stats(b):
                dve.wait_ge(x_in[b[1]], 16 * b[0] + 16)
                for t in range(T):
                    dve.bn_stats(stats[:, t, :], xs[b[1]][:, t, :]).then_inc(prep_step, 1)
                dve.wait_ge(prep_step, at(b, PREP_STEPS, PREP["STATS"]))
                dve.memset(hold[:], 0.0).then_inc(prep_step, 1)
                for t in range(T):
                    dve.bn_aggr(mv[:, t, :], stats[:, t, :]).then_inc(prep_step, 1)
                dve.wait_ge(prep_step, at(b, PREP_STEPS, PREP["VAR_IN"]))
                dve.tensor_scalar(vare[:], mv[:, :, 1], LN_EPS, None, ALU.add).then_inc(prep_step, 1)

            def rsqrt(b, y, v, t0, t1, base):
                dve.tensor_single_scalar(t0.bitcast(I32), v.bitcast(I32), 1, ALU.arith_shift_right).then_inc(prep_step, 1)
                dve.tensor_scalar(t1, v, -0.5, None, ALU.mult).then_inc(prep_step, 1)
                dve.wait_ge(prep_step, at(b, PREP_STEPS, base + 2))
                dve.tensor_scalar(y.bitcast(I32), t0.bitcast(I32), -1.0, float(RSQRT_MAGIC), ALU.mult, ALU.add)\
                   .then_inc(prep_step, 1)
                for n in range(NEWTON // 3):
                    dve.wait_ge(prep_step, at(b, PREP_STEPS, base + 3 + 3 * n))
                    dve.tensor_tensor(t0, y, y, ALU.mult).then_inc(prep_step, 1)
                    dve.wait_ge(prep_step, at(b, PREP_STEPS, base + 4 + 3 * n))
                    dve.tensor_tensor(t0, t0, t1, ALU.mult).then_inc(prep_step, 1)
                    dve.wait_ge(prep_step, at(b, PREP_STEPS, base + 5 + 3 * n))
                    dve.scalar_tensor_tensor(out=y, in0=t0, scalar=1.5, in1=y, op0=ALU.add, op1=ALU.mult)\
                       .then_inc(prep_step, 1)

            def ln_apply(b):
                dve.wait_ge(ln_rstd, at(b, 1, 1))
                for t in range(T):
                    dve.tensor_scalar(xn[:, t, :], xs[b[1]][:, t, :], mv[:, t, 0:1], rstd[:, t:t + 1],
                                                    ALU.subtract, ALU.mult).then_inc(prep_step, 1)

            def xnT_evacuate(b):
                dve.wait_ge(xnT_psum, at(b, 1, 1))
                dve.tensor_copy(xnT[:], misc[:, 0:S]).then_inc(misc_evacuated, 1)

            def xn_split(b, turn):
                dve.wait_ge(misc_evacuated, turn + 2)
                dve.tensor_copy(xnTh[b[1]][:], xnT[:]).then_inc(xn_high, 1)
                dve.wait_ge(xn_high, at(b, 1, 1))
                dve.tensor_tensor(xnTl[b[1]][:], xnT[:], xnTh[b[1]][:], ALU.subtract).then_inc(xn_low, 1)

            def proj_evacuate(b, turn):
                dve.wait_ge(proj_psum, at(b, 1, 1))
                dve.tensor_copy(proj[:].rearrange("p t n -> p (t n)"), misc[:, 0:T * NPROJ]).then_inc(misc_evacuated, 1)
                dve.wait_ge(misc_evacuated, turn + 2)
                qk = proj[:, :, 0:QKH * HD]
                dve.tensor_tensor(sq[:], qk, qk, ALU.mult).then_inc(prep_step, 1)
                lg = proj[:, :, NPROJ - NE:NPROJ]
                for t in range(T):
                    dve.max(top[:, t, :], lg[:, t, :]).then_inc(prep_step, 1)
                dve.wait_ge(prep_step, at(b, PREP_STEPS, PREP["SQUARES"]))
                dve.tensor_reduce(ms[:], sq[:].rearrange("p t (h e) -> p (t h) e", e=HD), AX.X, ALU.add).then_inc(prep_step, 1)
                for t in range(T):
                    dve.max_index(topi[:, t, :], top[:, t, :], lg[:, t, :]).then_inc(prep_step, 1)
                dve.wait_ge(prep_step, at(b, PREP_STEPS, PREP["SUMS"]))
                dve.tensor_scalar(ms[:], ms[:], 1.0 / HD, RMS_EPS, ALU.mult, ALU.add).then_inc(prep_step, 1)
                dve.tensor_tensor(ldiff[:], top[:, :, 1], top[:, :, 0], ALU.subtract).then_inc(prep_step, 1)
                dve.tensor_copy(topf[:], topi[:, :, 0:2]).then_inc(prep_step, 1)

            def head_rms(b):
                dve.wait_ge(prep_step, at(b, PREP_STEPS, PREP["TOPF"]))
                rsqrt(b, rinv[:], ms[:], rt0[:], rt1[:], PREP["TOPF"])

            def gates(b):
                dve.wait_ge(prep_exp, at(b, 1, 1))
                dve.tensor_scalar(wden[:], eldiff[:], 1.0, None, ALU.add).then_inc(prep_step, 1)
                dve.tensor_scalar(gden[:], egate[:], 1.0, None, ALU.add).then_inc(prep_step, 1)
                dve.wait_ge(prep_step, at(b, PREP_STEPS, PREP["DEN"]))
                dve.reciprocal(wtop[:, 0, :], wden[:]).then_inc(prep_step, 1)
                dve.reciprocal(gsig[:], gden[:]).then_inc(prep_step, 1)
                dve.wait_ge(prep_step, at(b, PREP_STEPS, PREP["WTOP0"]))
                dve.tensor_tensor(wtop[:, 1, :], wtop[:, 0, :], eldiff[:], ALU.mult).then_inc(prep_step, 1)
                for kb in range(2):
                    v = proj[:, kb, D + KV:D + 2 * KV].rearrange("p (g f d) -> p g f d", g=KVH, f=2)
                    s = gsig[:, kb, :].rearrange("p (g f d) -> p g f d", g=KVH, f=2)
                    dve.tensor_tensor(vw_view(b[1], kb, 0, HALF), v, s, ALU.mult).then_inc(v_ready, 1)
                dve.wait_ge(prep_step, at(b, PREP_STEPS, PREP["WTOP1"]))
                wide = [P, 2, T, NE]
                dve.tensor_tensor(chosen[:], chosen[:], wtop[:].unsqueeze(3).to_broadcast(wide), ALU.mult).then_inc(prep_step, 1)
                dve.wait_ge(prep_step, at(b, PREP_STEPS, PREP["WEIGHTED"]))
                dve.tensor_tensor(score[b[1]][:], chosen[:, 0], chosen[:, 1], ALU.add).then_inc(prep_step, 1)

            def output_scores(b):
                dve.wait_ge(prep_step, at(b, PREP_STEPS, PREP["SCORE"]))
                dve.tensor_scalar(yscore[b[1]][:], score[b[1]][:], y_scale[:, 0:1], None, ALU.mult).then_inc(prep_step, 1)

            def sT_evacuate(b):
                dve.wait_ge(sT_psum, at(b, 1, 1))
                dve.tensor_copy(scoreT[b[1]][:], misc[0:NE, 0:S]).then_inc(misc_evacuated, 1)

            def rotate(b):
                dve.wait_ge(prep_step, at(b, PREP_STEPS, PREP["RMS_INV"]))
                dve.tensor_tensor(rg[:], rinv[:], qmul[:].rearrange("p t h -> p (t h)"), ALU.mult).then_inc(prep_step, 1)
                dve.tensor_tensor(chosen[:], iota8[:].unsqueeze(1).unsqueeze(1).to_broadcast([P, 2, T, NE]),
                                  topf[:].rearrange("p t j -> p j t").unsqueeze(3).to_broadcast([P, 2, T, NE]),
                                  ALU.is_equal).then_inc(prep_step, 1)
                dve.wait_ge(prep_step, at(b, PREP_STEPS, PREP["RG"]))
                qk = proj[:, :, 0:QKH * HD].rearrange("p t (h e) -> p t h e", e=HD)
                rgb = rg[:].rearrange("p (t h) -> p t h", t=T).unsqueeze(3).to_broadcast([P, T, QKH, HD])
                dve.tensor_tensor(xr[:], qk, rgb, ALU.mult).then_inc(prep_step, 1)
                dve.wait_ge(prep_step, at(b, PREP_STEPS, PREP["XR"]))
                cosb = cos_sb[:].unsqueeze(2).to_broadcast([P, T, QKH, HD])
                dve.tensor_tensor(ra[:], xr[:], cosb, ALU.mult).then_inc(prep_step, 1)
                for f in range(2):
                    sinb = sin_sb[:, :, f * HALF:(f + 1) * HALF].unsqueeze(2).to_broadcast([P, T, QKH, HALF])
                    dve.tensor_tensor(rb[:, :, :, f * HALF:(f + 1) * HALF],
                                                xr[:, :, :, (1 - f) * HALF:(2 - f) * HALF], sinb, ALU.mult).then_inc(prep_step, 1)
                dve.wait_ge(prep_step, at(b, PREP_STEPS, PREP["ROT"]))
                dve.tensor_tensor(kf[:], ra[:, :, H:QKH, :], rb[:, :, H:QKH, :], ALU.add).then_inc(prep_step, 1)

            def k_parts(b):
                k4 = kf[:].rearrange("p t g (f d) -> p (t g f) d", f=2).unsqueeze(2).to_broadcast([P, T * GF, 2, HALF])
                kv = kp[:].rearrange("p t a (s z) d -> p (t a) s z d", s=2)
                kh, kl = kv[:, :, :, 0, :], kv[:, :, :, 1, :]
                dve.wait_ge(prep_step, at(b, PREP_STEPS, PREP["KF"]))
                dve.tensor_copy(kh, k4).then_inc(prep_step, 1)
                dve.wait_ge(prep_step, at(b, PREP_STEPS, PREP["K_HIGH"]))
                dve.tensor_tensor(kl, k4, kh, ALU.subtract).then_inc(prep_step, 1)

            def q_parts(b):
                for t in range(T):
                    qa, qb = (a[:, t, 0:H, :].rearrange("p (g r) e -> p g r e", g=KVH) for a in (ra, rb))
                    dve.tensor_tensor(qf[:, t].rearrange("p r g e -> p g r e"), qa, qb, ALU.add).then_inc(prep_step, 1)
                n = T * REP * GF
                q4 = qf[:].rearrange("p t r g (f d) -> p (t r g f) d", f=2).unsqueeze(2).to_broadcast([P, n, 2, HALF])
                qv = qp[:].rearrange("p t r a s d -> p (t r a) s d")
                dve.wait_ge(prep_step, at(b, PREP_STEPS, PREP["QF"]))
                dve.tensor_copy(qv[:, :, 0:2, :], q4).then_inc(prep_step, 1)
                dve.wait_ge(prep_step, at(b, PREP_STEPS, PREP["Q_HIGH"]))
                dve.tensor_tensor(qv[:, :, 2:4, :], q4, qv[:, :, 0:2, :], ALU.subtract).then_inc(prep_step, 1)

            def qT_evacuate(b):
                dve.wait_ge(qT_psum, at(b, 1, 1))
                dve.tensor_copy(qT[b[1]][:].rearrange("p r s -> p (r s)"), misc16[:, 0:REP * S]).then_inc(misc_evacuated, 1)

            def kT_evacuate(b):
                dve.wait_ge(kT_psum, at(b, 1, 1))
                dve.tensor_copy(kT[:], misc16[:, 0:S]).then_inc(misc_evacuated, 1)

            def k_padded(b, turn):
                dve.wait_ge(misc_evacuated, turn + 2)
                for gf in range(GF):
                    dve.tensor_scalar(kpad[b[1]][:, gf, :], kT[:], gfm_sb[:, gf:gf + 1], None, ALU.mult)\
                       .then_inc(k_ready, 1)

            def exact_maxima(b):
                with dve.If(general_path):
                    for n in range(ROUNDS):
                        dve.wait_ge(max_psum, at(b, ROUNDS + 1, n + 1))
                        t, gfs = (0, (2 * n, 2 * n + 1)) if n < 4 else (1, (n - 4,))
                        m = len(gfs) * REP
                        o = gfs[0] * REP
                        dve.tensor_reduce(nmax[:, t, o:o + m], sbank[0][:].rearrange("p (m w) -> p m w", m=m),
                                          AX.X, ALU.max, negate=True).then_inc(max_read, 1)
                    dve.wait_ge(max_psum, at(b, ROUNDS + 1, ROUNDS + 1))
                    dve.tensor_copy(nmaxT[:], sbank[0][0:32, 0:S]).then_inc(max_read, 1)

            def pv_evacuate(b):
                dve.wait_ge(pv_done, at(b, UNITS, UNITS + RING))
                dve.tensor_copy(pvs[:], pvbank[:]).then_inc(pv_evacuated, 1)

            def normalise(b):
                dve.wait_ge(pvT_psum, at(b, 1, 1))
                v = misc[:].rearrange("p (n e) -> p n e", e=8)
                dve.reciprocal(pinv[:], v[:, :, HALF]).then_inc(tail_step, 1)
                dve.wait_ge(tail_step, at(b, TAIL_STEPS, 1))
                dve.tensor_tensor(an[:].rearrange("p t (n d) -> p (t n) d", d=HALF), v[:, :, 0:HALF],
                                  pinv[:].unsqueeze(2).to_broadcast([P, 64, HALF]), ALU.mult).then_inc(misc_evacuated, 1)

            def aT_evacuate(b):
                dve.wait_ge(aT_psum, at(b, 1, 1))
                dve.tensor_copy(aT[:], misc[:, 0:S]).then_inc(misc_evacuated, 1)

            def final_add(b):
                dve.wait_ge(attn_psum, at(b, 1, 1))
                dve.wait_ge(comb_done, at(b, NE, NE + 1))
                dve.wait_ge(out_stored[b[1]], 16 * b[0] + 16)
                dve.tensor_tensor(ofin[b[1]][:].rearrange("p t d -> p (t d)"), misc[:, 0:S],
                                  acc[b[1]][:].rearrange("p t d -> p (t d)"), ALU.add).then_inc(misc_evacuated, 1)

            def combine(b, e):
                dve.wait_ge(y_psum, at(b, NE, e + 1 + H_RING))
                dve.wait_ge(comb_done, at(b, NE, e + 1))
                for t in range(T):
                    prior = xs[b[1]] if e == 0 else acc[b[1]]
                    last = dve.scalar_tensor_tensor(out=acc[b[1]][:, t, :], in0=ybank[:, t * P:(t + 1) * P],
                                                    scalar=yscore[b[1]][:, t, e:e + 1], in1=prior[:, t, :],
                                                    op0=ALU.mult, op1=ALU.add)
                last.then_inc(comb_done, 1)

            def combines(b, prv, k):
                for half in (2 * k - 2, 2 * k - 1):
                    if half in EXPERT_OUT_HALVES:
                        combine(b, EXPERT_OUT_HALVES.index(half))
                    if prv is not None and half >= 0 and half + HALVES in EXPERT_OUT_HALVES:
                        combine(prv, EXPERT_OUT_HALVES.index(half + HALVES))

            def tail(b, k):
                if k == TAIL_SLOTS["a_t"] + 1:
                    aT_evacuate(b)
                if k == TAIL_SLOTS["attn_out"] + 1:
                    final_add(b)

            def prepare(b, cur, prv, k):
                if k == PREP_SLOTS["xn_t"] + 1:
                    xnT_evacuate(b)
                    xn_split(b, misc_turn("xn_t", cur, prv is not None, True))
                if k == PREP_SLOTS["proj"] + 1:
                    proj_evacuate(b, misc_turn("proj", cur, prv is not None, True))
                if k == 4:
                    head_rms(b)
                if k == 5:
                    rotate(b)
                if k == 6:
                    k_parts(b)
                    q_parts(b)
                if k == PREP_SLOTS["k_t"] + 1:
                    kT_evacuate(b)
                if k == 8:
                    gates(b)
                    output_scores(b)
                if k == PREP_SLOTS["q_t"] + 1:
                    qT_evacuate(b)
                if k == 9:
                    k_padded(b, misc_turn("k_t", cur, prv is not None, True))
                if k == PREP_SLOTS["score_t"] + 1:
                    sT_evacuate(b)
                    exact_maxima(b)

            def seq(b, nxt, prv):
                for k in range(UNITS + 1):
                    if k == 0:
                        if nxt is not None:
                            ln_stats(nxt)
                        if prv is not None:
                            pv_evacuate(prv)
                            normalise(prv)
                        if nxt is not None:
                            ln_apply(nxt)
                    if prv is not None:
                        tail(prv, k)
                    combines(b, prv if k <= UNITS - 1 else None, k)
                    if nxt is not None:
                        prepare(nxt, b, prv, k)

            general_path = dve.value_load(big_i[0:1, 0:1], min_val=0, max_val=1)
            first = (0, 0)
            ln_stats(first)
            ln_apply(first)
            xnT_evacuate(first)
            xn_split(first, misc_turn("xn_t", None, False, True))
            proj_evacuate(first, misc_turn("proj", None, False, True))
            head_rms(first)
            rotate(first)
            k_parts(first)
            q_parts(first)
            gates(first)
            kT_evacuate(first)
            k_padded(first, misc_turn("k_t", None, False, True))
            qT_evacuate(first)
            sT_evacuate(first)
            dve.wait_ge(experts_in, EXPERTS)
            for j, w in enumerate((w1_sb[:].rearrange("p e h -> p (e h)"), w2_sb[:].rearrange("p e c d -> p (e c d)"),
                                   b1_sb[:].rearrange("p e c -> p (e c)"))):
                dve.tensor_reduce(peak[:, j:j + 1], w, AX.X, ALU.max, apply_absolute_value=True).then_inc(setup, 1)
            dve.memset(ones3[:], 1.0).then_inc(setup, 1)
            dve.wait_ge(peak_psum, 1)
            dve.tensor_reduce(peak_all[:], hbank[0:3, 0, 0:P], AX.X, ALU.max).then_inc(setup, 1)
            dve.wait_ge(setup, 39)
            dve.tensor_scalar(peak_diag[:], id32[0:3, 0:3], peak_all[:, 0:1], None, ALU.mult).then_inc(setup, 1)
            dve.wait_ge(peak_psum, 2)
            dve.tensor_copy(bound[:], hbank[:, 1, 0:3]).then_inc(setup, 1)
            dve.wait_ge(setup, 41)
            dve.scalar_tensor_tensor(out=bound[:, 2:3], in0=bound[:, 0:1], scalar=float(D), in1=bound[:, 2:3],
                                     op0=ALU.mult, op1=ALU.add).then_inc(setup, 1)
            dve.wait_ge(setup, 42)
            dve.tensor_scalar(bound[:], bound[:], TINY_MAX, None, ALU.max).then_inc(setup, 1)
            dve.wait_ge(setup, 43)
            dve.tensor_single_scalar(bound_e[:], bound[:].bitcast(I32), 23, ALU.arith_shift_right).then_inc(setup, 1)
            dve.wait_ge(setup, 44)
            dve.tensor_scalar(up[:].bitcast(I32), bound_e[:], -float(EXP_BIT), float((254 + F16_TOP) * EXP_BIT),
                              ALU.mult, ALU.add).then_inc(setup, 1)
            dve.tensor_scalar(down[:].bitcast(I32), bound_e[:], -float(F16_TOP), float(EXP_BIT),
                              ALU.add, ALU.mult).then_inc(setup, 1)
            dve.wait_ge(setup, 46)
            dve.tensor_tensor(h_scale[:], down[:, 0:1], up[:, 2:3], ALU.mult).then_inc(setup, 1)
            dve.tensor_tensor(y_scale[:], down[:, 1:2], down[:, 2:3], ALU.mult).then_inc(setup, 1)
            dve.tensor_scalar(b1s[:], b1_sb[:], up[:, 2:3], None, ALU.mult).then_inc(setup, 1)
            dve.wait_ge(setup, SETUP_STEPS)
            output_scores(first)
            for n, (low, w, high) in enumerate(((w1l, w1_sb, w1h), (w2l, w2_sb, w2h))):
                dve.wait_ge(w_high, n + 1)
                dve.scalar_tensor_tensor(out=low[:], in0=w[:], scalar=up[:, n:n + 1], in1=high[:],
                                         op0=ALU.mult, op1=ALU.subtract).then_inc(w_split, 1)
            exact_maxima(first)
            schedule(dve, seq)
            for e in LATE_EXPERTS:
                combine(LAST, e)
            pv_evacuate(LAST)
            normalise(LAST)
            aT_evacuate(LAST)
            final_add(LAST)


def tables():
    pos = np.arange(S, dtype=np.float32)
    angles = np.arange(0, HD, 2, dtype=np.float32) / np.float32(HD) * np.float32(math.pi)
    radius = np.float32(1.0) / (np.float32(1.0) + pos[:, None] * np.float32(0.01))
    ang = pos[:, None] * angles[None, :]
    cos, sin = radius * np.cos(ang), radius * np.sin(ang)
    cos_t = np.concatenate([cos, cos], 1).reshape(T, P, HD).transpose(1, 0, 2)
    sin_t = np.concatenate([sin, -sin], 1).reshape(T, P, HD).transpose(1, 0, 2)
    gf_mask = (np.arange(P)[:, None] // 16 == np.arange(GF)[None, :]).astype(np.float32)
    ident = np.eye(P, dtype=np.float32)
    causal = np.where(np.arange(P)[None, :] > np.arange(P)[:, None], NEG, 0.0).astype(np.float32)
    return cos_t, sin_t, gf_mask, ident, causal


def kernel(L0_attn_x, L0_attn_Wq, L0_attn_Wk, L0_attn_Wv, L0_attn_Wg, L0_attn_Wo, L0_attn_q_gain,
           L0_attn_lambda_param, L0_ffn_Wg, L0_ffn_W1, L0_ffn_b1, L0_ffn_W2, L0_ffn_b2):
    import concourse.bacc as _bacc
    from concourse.bass_utils import run_bass_kernel_spmd as _run

    a = np.asarray
    cos_t, sin_t, gf_mask, ident, causal = tables()
    w_proj = np.concatenate([a(L0_attn_Wq).T, a(L0_attn_Wk).T, a(L0_attn_Wv).T, a(L0_attn_Wg).T, a(L0_ffn_Wg)], axis=1)
    wo = a(L0_attn_Wo).T.reshape(KVH, REP, 2, HALF, D).transpose(2, 1, 0, 3, 4).reshape(2, D // 2, D)
    lam = np.repeat(a(L0_attn_lambda_param).reshape(KVH, REP).T.reshape(H), HALF)[:, None]
    arrays = {
        "x": a(L0_attn_x),
        "w_proj": w_proj,
        "wo_a": np.concatenate([wo[0], wo[0]]),
        "wo_b": np.concatenate([wo[1], wo[1]]),
        "gain": np.broadcast_to(a(L0_attn_q_gain)[None, :], (P, H)),
        "lam_col": np.concatenate([np.ones((D // 2, 1), np.float32), lam]),
        "w1": a(L0_ffn_W1).transpose(1, 0, 2),
        "b1": a(L0_ffn_b1).reshape(NE, HC, P).transpose(2, 0, 1),
        "w2": a(L0_ffn_W2).reshape(NE, HC, P, D).transpose(2, 0, 1, 3),
        "b2": a(L0_ffn_b2),
        "cos_t": cos_t,
        "sin_t": sin_t,
        "gf_mask": gf_mask,
        "ident": ident,
        "causal_neg": causal,
    }
    arrays = {n: np.ascontiguousarray(v) for n, v in arrays.items()}
    nc = _bacc.Bacc("TRN2", target_bir_lowering=False, num_devices=1)
    args = {n: nc.dram_tensor(f"in_{n}", v.shape, mybir.dt.from_np(v.dtype), kind="ExternalInput").ap()
            for n, v in arrays.items()}
    out = nc.dram_tensor("out_y", (NB, S, D), F32, kind="ExternalOutput").ap()
    moe_attention_kernel(nc, out=out, **args)
    r = _run(nc, [{f"in_{n}": v for n, v in arrays.items()}], core_ids=[0])
    return r.results[0]["out_y"]
```
